# Optimizing a Trainium2 kernel written in Bass

```python
import numpy as np
import jax
import jax.numpy as jnp

def _softmax(x, axis=-1):
    return jax.nn.softmax(x, axis=axis)

def _gelu(x):
    return jax.nn.gelu(x, approximate=True)

def _silu(x):
    return jax.nn.silu(x)

def _sigmoid(x):
    return jax.nn.sigmoid(x)

def _layernorm(x, axis=-1, eps=1e-05):
    m = jnp.mean(x, axis=axis, keepdims=True)
    v = jnp.var(x, axis=axis, keepdims=True)
    return (x - m) / jnp.sqrt(v + eps)

def _scatter_add(tgt, idx, src, axis=0):
    return tgt.at[idx].add(src)

def _segment_sum(src, seg, n):
    return jax.ops.segment_sum(src, seg, n)
kernel_name = 'mk_conv_seq_d1_conv_nchw256_r2_31b3e3'

def setup_inputs(seed: int=0):
    np.random.seed(seed)
    _w = jnp.asarray

    def _rec_inputs():
        import jax
        import jax.numpy as jnp
        _gk = jax.random.key(seed)
        x = 7.22e-05 + 1 * jax.random.normal(jax.random.fold_in(_gk, 1), (8, 128, 32, 32), jnp.float32)
        return x
    x = _rec_inputs()

    def _L0_conv_setup():
        import jax, jax.numpy as jnp
        import numpy as np
        BN_EPS = 1e-05
        key = jax.random.key(seed)
        ks = jax.random.split(key, 8)
        B, C, H, W = (8, 128, 32, 32)
        Ci = 64
        s_in = 1.0 / np.sqrt(C)
        s_int = 1.0 / np.sqrt(Ci)
        return {'x': jax.random.normal(ks[0], (B, C, H, W), jnp.float32), 'w_g': jax.random.normal(ks[1], (Ci, C), jnp.float32) * s_in, 'b_g': jnp.zeros((Ci,), jnp.float32), 'w_theta': jax.random.normal(ks[2], (Ci, C), jnp.float32) * s_in, 'b_theta': jnp.zeros((Ci,), jnp.float32), 'w_phi': jax.random.normal(ks[3], (Ci, C), jnp.float32) * s_in, 'b_phi': jnp.zeros((Ci,), jnp.float32), 'w_out': jax.random.normal(ks[4], (C, Ci), jnp.float32) * s_int, 'b_out': jnp.zeros((C,), jnp.float32), 'bn_gamma': jnp.ones((C,), jnp.float32), 'bn_beta': jnp.zeros((C,), jnp.float32), 'bn_mean': jnp.zeros((C,), jnp.float32), 'bn_var': jnp.ones((C,), jnp.float32)}
    _L0_conv_all = _L0_conv_setup()
    _L0_conv_in = {k: v for k, v in _L0_conv_all.items() if k in ('w_g', 'b_g', 'w_theta', 'b_theta', 'w_phi', 'b_phi', 'w_out', 'b_out', 'bn_gamma', 'bn_beta', 'bn_mean', 'bn_var')}
    del _L0_conv_all
    return {'x': x, 'L0_conv_w_g': _L0_conv_in['w_g'], 'L0_conv_b_g': _L0_conv_in['b_g'], 'L0_conv_w_theta': _L0_conv_in['w_theta'], 'L0_conv_b_theta': _L0_conv_in['b_theta'], 'L0_conv_w_phi': _L0_conv_in['w_phi'], 'L0_conv_b_phi': _L0_conv_in['b_phi'], 'L0_conv_w_out': _L0_conv_in['w_out'], 'L0_conv_b_out': _L0_conv_in['b_out'], 'L0_conv_bn_gamma': _L0_conv_in['bn_gamma'], 'L0_conv_bn_beta': _L0_conv_in['bn_beta'], 'L0_conv_bn_mean': _L0_conv_in['bn_mean'], 'L0_conv_bn_var': _L0_conv_in['bn_var']}

def reference(x, L0_conv_w_g, L0_conv_b_g, L0_conv_w_theta, L0_conv_b_theta, L0_conv_w_phi, L0_conv_b_phi, L0_conv_w_out, L0_conv_b_out, L0_conv_bn_gamma, L0_conv_bn_beta, L0_conv_bn_mean, L0_conv_bn_var):
    import jax
    import jax.numpy as jnp

    def _L0_conv_ref(x, w_g, b_g, w_theta, b_theta, w_phi, b_phi, w_out, b_out, bn_gamma, bn_beta, bn_mean, bn_var):
        import jax, jax.numpy as jnp
        import numpy as np
        BN_EPS = 1e-05
        B, C, H, W = x.shape
        Ci = w_g.shape[0]
        N = H * W
        g = (jnp.einsum('bchw,oc->bhwo', x, w_g) + b_g).reshape(B, N, Ci)
        theta = (jnp.einsum('bchw,oc->bhwo', x, w_theta) + b_theta).reshape(B, N, Ci)
        phi = (jnp.einsum('bchw,oc->bohw', x, w_phi) + b_phi[:, None, None]).reshape(B, Ci, N)
        att = jax.nn.softmax(jnp.einsum('bnc,bcm->bnm', theta, phi), axis=-1)
        y = jnp.einsum('bnm,bmc->bnc', att, g).reshape(B, H, W, Ci)
        out = jnp.einsum('bhwc,oc->bohw', y, w_out) + b_out[:, None, None]
        inv = bn_gamma / jnp.sqrt(bn_var + BN_EPS)
        out = out * inv[:, None, None] + (bn_beta - bn_mean * inv)[:, None, None]
        return x + out

    def _gn(v, G=32, eps=1e-05):
        B_, C_, H_, W_ = v.shape
        g = v.reshape(B_, G, C_ // G, H_, W_)
        m = jnp.mean(g, axis=(2, 3, 4), keepdims=True)
        s = jnp.var(g, axis=(2, 3, 4), keepdims=True)
        return ((g - m) / jnp.sqrt(s + eps)).reshape(v.shape)

    def _ln_c(v, eps=1e-06):
        m = jnp.mean(v, axis=1, keepdims=True)
        s = jnp.var(v, axis=1, keepdims=True)
        return (v - m) / jnp.sqrt(s + eps)

    def _ln_t(v, eps=1e-05):
        m = jnp.mean(v, axis=-1, keepdims=True)
        s = jnp.var(v, axis=-1, keepdims=True)
        return (v - m) / jnp.sqrt(s + eps)

    def _to_tokens(v):
        B_, C_, H_, W_ = v.shape
        return v.reshape(B_, C_, H_ * W_).transpose(0, 2, 1)

    def _from_tokens(t, like):
        B_, C_, H_, W_ = like.shape
        return t.transpose(0, 2, 1).reshape(B_, C_, H_, W_)
    x = _L0_conv_ref(x, L0_conv_w_g, L0_conv_b_g, L0_conv_w_theta, L0_conv_b_theta, L0_conv_w_phi, L0_conv_b_phi, L0_conv_w_out, L0_conv_b_out, L0_conv_bn_gamma, L0_conv_bn_beta, L0_conv_bn_mean, L0_conv_bn_var)
    return x

_drawn_inputs = setup_inputs


def setup_inputs(seed=0):
    import zlib

    import numpy as np

    out = dict(_drawn_inputs(seed))
    spreads = {'L0_conv_b_g': (0.0, 0.1),
     'L0_conv_b_theta': (0.0, 0.1),
     'L0_conv_b_phi': (0.0, 0.1),
     'L0_conv_b_out': (0.0, 0.1),
     'L0_conv_bn_gamma': (1.0, 0.2),
     'L0_conv_bn_beta': (0.0, 0.1),
     'L0_conv_bn_mean': (0.0, 0.1),
     'L0_conv_bn_var': (1.0, 0.2)}
    factors = {}
    for name, (base, spread) in spreads.items():
        noise = np.random.default_rng([zlib.crc32(name.encode()), seed]).standard_normal(out[name].shape)
        drawn = base * np.exp(spread * noise) if base else spread * noise
        out[name] = jnp.asarray(drawn.astype(out[name].dtype))
    for name, factor in factors.items():
        out[name] = (out[name] * factor).astype(out[name].dtype)
    return out
```

```python
def build_nonlocal_attention(nc, x, w_qk_t, w_g_t, w_out_t, channel_vectors, out):
    from contextlib import ExitStack

    import concourse.bass as bass
    from concourse import mybir

    F32 = mybir.dt.float32
    F32R = mybir.dt.float32r
    F16 = mybir.dt.float16
    ALU = mybir.AluOpType
    ACT = mybir.ActivationFunctionType
    AX = mybir.AxisListType

    B, C, H, W = x.shape
    N = H * W
    CI = w_g_t.shape[1]
    P = 128
    BANK = 512
    EPS = 1e-5
    PROB_SCALE = 2.0 ** 15
    G_TOP = 2.0 ** 14
    G_LEAST = 1e-30

    MT = N // P
    TILES = B * MT
    HALF_TILES = BANK // P
    HALVES = TILES // HALF_TILES
    PER_IMAGE = N // BANK
    STEPS = 2 * MT
    LAG = 12
    assert (C, CI, MT, PER_IMAGE, HALF_TILES) == (P, P // 2, 8, 2, 4) and B % 2 == 0

    x_v = x.rearrange("b c h w -> c b (h w)")
    out_v = out.rearrange("b c h w -> c b (h w)")

    with ExitStack() as ctx:
        def sbuf(name, shape, dt):
            return ctx.enter_context(nc.sbuf_tensor(name, shape, dt))

        def psum(name, shape, dt=F32):
            return ctx.enter_context(nc.psum_tensor(name, shape, dt))

        def sem(name):
            return ctx.enter_context(nc.semaphore(name))

        wqk = sbuf("wqk", [P, P], F32)
        wg = sbuf("wg", [P, CI], F32)
        wout = sbuf("wout", [P, C + 1], F32)
        vec = sbuf("vec", [P, 6], F32)
        ident = sbuf("ident", [P, P], F32)
        bn = sbuf("bn", [P, 8], F32)
        BIAS_QK, B_OUT, GAMMA, BETA, MEAN, VAR = (vec[:, i:i + 1] for i in range(6))
        VAR_EPS, STD, RSTD, INV, MEAN_INV, BETA_SHIFT, BIAS_SUM, SHIFT = (bn[:, i:i + 1] for i in range(8))

        x_in = [sbuf(f"x_in{i}", [P, N], F32) for i in range(2)]
        qk = sbuf("qk", [P, N], F32)
        hi = [sbuf(f"hi{i}", [P, N], F32R) for i in range(2)]
        lo = [sbuf(f"lo{i}", [P, N], F32R) for i in range(2)]
        hi_sw = [sbuf(f"hi_sw{i}", [P, N], F32R) for i in range(2)]
        lo_sw = [sbuf(f"lo_sw{i}", [P, N], F32R) for i in range(2)]
        g_raw = sbuf("g_raw", [P, MT, CI], F32)
        g_scaled = sbuf("g_scaled", [P, MT, CI], F32)
        g_parts = [sbuf(f"g_parts{i}", [P, MT, 2 * CI], F16) for i in range(2)]
        g_peak = sbuf("g_peak", [P, 2], F32)
        g_peak_all = sbuf("g_peak_all", [P, 2], F32)
        g_unit = sbuf("g_unit", [P, 2], F32)
        g_factor = sbuf("g_factor", [P, 2], F32)
        resid = [sbuf(f"resid{i}", [P, N], F32) for i in range(2)]

        probs = [sbuf(f"probs{i}", [P, N], F32) for i in range(2)]
        neg_max = sbuf("neg_max", [P, STEPS], F32)
        row_sum = sbuf("row_sum", [P, STEPS], F32)
        inv_sum = sbuf("inv_sum", [P, STEPS], F32)
        row_scale = sbuf("row_scale", [P, STEPS], F32)
        pt_hi = [sbuf(f"pt_hi{i}", [P, MT, BANK], F16) for i in range(2)]
        pt_lo = [sbuf(f"pt_lo{i}", [P, MT, BANK], F16) for i in range(2)]
        scale_row = sbuf("scale_row", [P, BANK], F32)
        y_norm = sbuf("y_norm", [P, BANK], F32)

        ps_scores = [psum(f"ps_scores{i}", [P, N]) for i in range(2)]
        ps_flip = [psum(f"ps_flip{i}", [P, BANK]) for i in range(2)]
        ps_y = psum("ps_y", [P, BANK])
        ps_misc = psum("ps_misc", [P, BANK])

        weights_in = sem("weights_in")
        x_arrived = [sem(f"x_arrived{i}") for i in range(2)]
        swapped = [sem(f"swapped{i}") for i in range(2)]
        stored = [sem(f"stored{i}") for i in range(2)]
        ident_zero = sem("ident_zero")
        ident_ready = sem("ident_ready")
        bn_step = sem("bn_step")
        bn_std = sem("bn_std")
        g_bias_ready = sem("g_bias_ready")
        shift_ready = sem("shift_ready")
        proj_ready = sem("proj_ready")
        proj_out = sem("proj_out")
        hi_ready = sem("hi_ready")
        lo_ready = sem("lo_ready")
        g_ready = sem("g_ready")
        g_out = sem("g_out")
        g_peak_ready = sem("g_peak_ready")
        g_peak_everywhere = sem("g_peak_everywhere")
        g_unit_ready = sem("g_unit_ready")
        g_factor_ready = sem("g_factor_ready")
        g_hi_ready = sem("g_hi_ready")
        g_scaled_ready = sem("g_scaled_ready")
        g_split = sem("g_split")
        resid_ready = sem("resid_ready")
        scores_ready = sem("scores_ready")
        max_ready = sem("max_ready")
        probs_ready = sem("probs_ready")
        flipped = sem("flipped")
        pt_hi_ready = sem("pt_hi_ready")
        pt_lo_ready = sem("pt_lo_ready")
        y_ready = sem("y_ready")
        inv_sum_ready = sem("inv_sum_ready")
        row_scale_ready = sem("row_scale_ready")
        spread_ready = sem("spread_ready")
        spread_out = sem("spread_out")
        y_scaled = sem("y_scaled")
        conv_ready = sem("conv_ready")
        result_ready = sem("result_ready")

        block = ctx.enter_context(nc.Block())

        def tile_at(it, k):
            return it * STEPS + k

        def half_at(it, k):
            return it * (STEPS // HALF_TILES) + k // HALF_TILES

        def image_at(it, k):
            return it * (STEPS // MT) + k // MT

        def exists(index, count):
            return not isinstance(index, int) or 0 <= index < count

        def wait(eng, semaphore, value):
            if not isinstance(value, int) or value > 0:
                eng.wait_ge(semaphore, value)

        def run_steps(eng, step):
            for k in range(MT):
                step(0, k)
            with eng.Fori(0, B // 2 - 1) as it:
                for k in range(MT, MT + STEPS):
                    step(it, k)
            for k in range(MT, STEPS + LAG):
                step(B // 2 - 1, k)

        @block.sync
        def _(sp):
            sp.dma_start(x_in[0][:, :], x_v[:, 0, :]).then_inc(x_arrived[0], 16)
            sp.dma_start(wqk[:, :], w_qk_t).then_inc(weights_in, 16)
            sp.dma_start(wg[:, :], w_g_t).then_inc(weights_in, 16)
            sp.dma_start(wout[0:CI, :], w_out_t).then_inc(weights_in, 16)
            sp.dma_start(wout[CI:P, :], w_out_t).then_inc(weights_in, 16)
            sp.dma_start(vec[:, :], channel_vectors).then_inc(weights_in, 16)
            sp.dma_start(x_in[1][:, :], x_v[:, 1, :]).then_inc(x_arrived[1], 16)

            def store(it, k):
                h = half_at(it, k)
                if not exists(h, HALVES):
                    return
                part = (k // HALF_TILES) % PER_IMAGE
                ring = (k // MT) % 2
                sp.wait_ge(result_ready, h + 1)
                cols = slice(part * BANK, (part + 1) * BANK)
                dst = out_v[:, image_at(it, k), cols] if isinstance(h, int) else \
                    out_v[:, bass.ds(image_at(it, k), 1), cols]
                sp.dma_start(dst, resid[ring][:, cols]).then_inc(stored[ring], 16)

            def image(it, k):
                b, r = image_at(it, k), (k // MT) % 2
                store(it, k - 2 * MT)
                sp.wait_ge(hi_ready, b + 1)
                sp.dma_start(hi_sw[r][0:CI, :].bitcast(F32), hi[r][CI:P, :].bitcast(F32)).then_inc(swapped[r], 16)
                sp.dma_start(hi_sw[r][CI:P, :].bitcast(F32), hi[r][0:CI, :].bitcast(F32)).then_inc(swapped[r], 16)
                sp.wait_ge(lo_ready, b + 1)
                sp.dma_start(lo_sw[r][0:CI, :].bitcast(F32), lo[r][CI:P, :].bitcast(F32)).then_inc(swapped[r], 16)
                sp.dma_start(lo_sw[r][CI:P, :].bitcast(F32), lo[r][0:CI, :].bitcast(F32)).then_inc(swapped[r], 16)
                store(it, k - 2 * MT + HALF_TILES)
                if exists(b + 2, B):
                    sp.wait_ge(proj_ready, 2 * b + 2)
                    sp.wait_ge(g_ready, b + 1)
                    sp.wait_ge(resid_ready, b + 1)
                    src = x_v[:, b + 2, :] if isinstance(b, int) else x_v[:, bass.ds(b + 2, 1), :]
                    sp.dma_start(x_in[r][:, :], src).then_inc(x_arrived[r], 16)

            image(0, 0)
            image(0, MT)
            with sp.Fori(1, B // 2 - 1) as it:
                image(it, 0)
                image(it, MT)
            image(B // 2 - 1, 0)
            image(B // 2 - 1, MT)
            for k in range(0, STEPS, HALF_TILES):
                store(B // 2 - 1, k)
            for r in range(2):
                sp.wait_ge(stored[r], 16 * HALVES // 2)

        @block.gpsimd
        def _(pool):
            nc.gpsimd.memset(ident[:, :], 0.0).then_inc(ident_zero, 1)
            pool.wait_ge(ident_zero, 1)
            nc.gpsimd.affine_select(out=ident[:, :], in_=ident[:, :], compare_op=ALU.not_equal, fill=1.0,
                                    base=0, pattern=[[-1, P]], channel_multiplier=1).then_inc(ident_ready, 1)

            def image(b):
                r = b % 2
                pool.wait_ge(proj_out, 2 * b + 2)
                wait(pool, scores_ready, (b - 1) * MT)
                nc.gpsimd.tensor_scalar(out=hi[r][:, :], in0=qk[:, :], scalar1=1.0, scalar2=0.0,
                                        op0=ALU.mult, op1=ALU.add).then_inc(hi_ready, 1)
                pool.wait_ge(hi_ready, b + 1)
                nc.gpsimd.tensor_tensor(lo[r][:, :], qk[:, :], hi[r][:, :].bitcast(F32),
                                        ALU.subtract).then_inc(lo_ready, 1)
                pool.wait_ge(g_peak_ready, b + 1)
                nc.gpsimd.partition_all_reduce(g_peak_all[:, r:r + 1], g_peak[:, r:r + 1], P,
                                               bass.bass_isa.ReduceOp.max).then_inc(g_peak_everywhere, 1)
                pool.wait_ge(g_factor_ready, b + 1)
                wait(pool, y_ready, (b - 1) * PER_IMAGE)
                nc.gpsimd.tensor_scalar(out=g_parts[r][:, :, 0:CI], in0=g_raw[:, :, :],
                                        scalar1=g_factor[:, r:r + 1], scalar2=1.0,
                                        op0=ALU.mult, op1=ALU.mult).then_inc(g_hi_ready, 1)
                nc.gpsimd.tensor_scalar(out=g_scaled[:, :, :], in0=g_raw[:, :, :],
                                        scalar1=g_factor[:, r:r + 1], scalar2=1.0,
                                        op0=ALU.mult, op1=ALU.mult).then_inc(g_scaled_ready, 1)
                pool.wait_ge(g_hi_ready, b + 1)
                pool.wait_ge(g_scaled_ready, b + 1)
                nc.gpsimd.tensor_tensor(g_parts[r][:, :, CI:2 * CI], g_scaled[:, :, :],
                                        g_parts[r][:, :, 0:CI], ALU.subtract).then_inc(g_split, 1)
                pool.wait_ge(shift_ready, 1)
                pool.wait_ge(x_arrived[r], 16 * (b // 2 + 1))
                wait(pool, stored[r], 16 * PER_IMAGE * (b // 2))
                nc.gpsimd.tensor_scalar(out=resid[r][:, :], in0=x_in[r][:, :], scalar1=SHIFT, scalar2=1.0,
                                        op0=ALU.add, op1=ALU.mult).then_inc(resid_ready, 1)

            for b in range(B):
                image(b)

        @block.scalar
        def _(act):
            def evacuate_projection(b, c, source):
                act.wait_ge(proj_ready, 2 * b + c + 1)
                wait(act, lo_ready, b)
                nc.scalar.activation(qk[:, c * BANK:(c + 1) * BANK], source[:, :], ACT.Identity,
                                     bias=BIAS_QK).then_inc(proj_out, 1)

            def evacuate_g(b, source):
                act.wait_ge(g_ready, b + 1)
                wait(act, g_split, b)
                nc.scalar.activation(g_raw[:, :, :].rearrange("p t c -> p (t c)"), source[:, :],
                                     ACT.Copy).then_inc(g_out, 1)

            act.wait_ge(bn_step, 1)
            nc.scalar.activation(STD, VAR_EPS, ACT.Sqrt).then_inc(bn_std, 1)
            act.wait_ge(weights_in, 80)
            evacuate_projection(0, 0, ps_misc)
            evacuate_projection(0, 1, ps_y)
            evacuate_g(0, ps_flip[0])

            def step(it, k):
                image, j = image_at(it, k), k % MT
                h = half_at(it, k - 9)
                if j % HALF_TILES == 1 and exists(h, HALVES):
                    act.wait_ge(spread_ready, h + 1)
                    wait(act, y_scaled, h)
                    nc.scalar.activation(scale_row[:, :], ps_misc[:, :], ACT.Copy).then_inc(spread_out, 1)
                if j in (2, 4) and exists(image + 1, B):
                    evacuate_projection(image + 1, j // 2 - 1, ps_misc)
                if j == 6 and exists(image + 1, B):
                    evacuate_g(image + 1, ps_misc)
                t = tile_at(it, k - 2)
                if exists(t, TILES):
                    slot, ring = (k - 2) % HALF_TILES, (k - 2) // HALF_TILES % 2
                    if slot == 0:
                        wait(act, y_ready, half_at(it, k - 2) - 1)
                    for c in range(2):
                        act.wait_ge(flipped, 2 * t + c + 1)
                        nc.scalar.activation(
                            pt_hi[ring][:, c * HALF_TILES:(c + 1) * HALF_TILES, slot * P:(slot + 1) * P],
                            ps_flip[c][:, :].rearrange("p (a n) -> p a n", n=P),
                            ACT.Copy, scale=PROB_SCALE).then_inc(pt_hi_ready, 1)
                t = tile_at(it, k)
                if exists(t, TILES):
                    act.wait_ge(max_ready, t + 1)
                    wait(act, flipped, 2 * t - 2)
                    nc.scalar.activation(probs[k % 2][:, :], ps_scores[k % 2][:, :], ACT.Exp,
                                         bias=neg_max[:, k % STEPS:k % STEPS + 1],
                                         accum_out=row_sum[:, k % STEPS:k % STEPS + 1]).then_inc(probs_ready, 1)

            run_steps(act, step)

        @block.vector
        def _(dve):
            dve.wait_ge(weights_in, 80)
            nc.vector.tensor_scalar(out=VAR_EPS, in0=VAR, scalar1=EPS, scalar2=None,
                                    op0=ALU.add).then_inc(bn_step, 1)
            dve.wait_ge(bn_std, 1)
            nc.vector.reciprocal(RSTD, STD).then_inc(bn_step, 1)
            dve.wait_ge(bn_step, 2)
            nc.vector.tensor_tensor(INV, GAMMA, RSTD, ALU.mult).then_inc(bn_step, 1)
            dve.wait_ge(bn_step, 3)
            nc.vector.tensor_tensor(MEAN_INV, MEAN, INV, ALU.mult).then_inc(bn_step, 1)
            dve.wait_ge(bn_step, 4)
            nc.vector.tensor_tensor(BETA_SHIFT, BETA, MEAN_INV, ALU.subtract).then_inc(bn_step, 1)

            def peak_of_g(b, r):
                dve.wait_ge(g_out, b + 1)
                nc.vector.tensor_reduce(out=g_peak[:, r:r + 1], in_=g_raw[:, :, :], op=ALU.max, axis=AX.XY,
                                        apply_absolute_value=True).then_inc(g_peak_ready, 1)

            def row_maximum(t, k):
                dve.wait_ge(scores_ready, t + 1)
                nc.vector.tensor_reduce(out=neg_max[:, k % STEPS:k % STEPS + 1], in_=ps_scores[k % 2][:, :],
                                        op=ALU.max, axis=AX.X, negate=True).then_inc(max_ready, 1)

            peak_of_g(0, 0)
            dve.wait_ge(g_bias_ready, 1)
            nc.vector.tensor_tensor(BIAS_SUM, ps_flip[1][:, 0:1], B_OUT, ALU.add).then_inc(bn_step, 1)
            dve.wait_ge(bn_step, 6)
            nc.vector.scalar_tensor_tensor(out=SHIFT, in0=BIAS_SUM, scalar=INV, in1=BETA_SHIFT,
                                           op0=ALU.mult, op1=ALU.add).then_inc(shift_ready, 1)
            row_maximum(0, 0)

            def step(it, k):
                image, j = image_at(it, k), k % MT
                h = half_at(it, k - 10)
                if j % HALF_TILES == 2 and exists(h, HALVES):
                    dve.wait_ge(y_ready, h + 1)
                    dve.wait_ge(spread_out, h + 1)
                    wait(dve, conv_ready, h)
                    nc.vector.tensor_tensor(y_norm[:, :], ps_y[:, :], scale_row[:, :],
                                            ALU.mult).then_inc(y_scaled, 1)
                h = half_at(it, k - 11)
                if j % HALF_TILES == 3 and exists(h, HALVES):
                    ring, part = (k - 11) // MT % 2, (k - 11) // HALF_TILES % PER_IMAGE
                    dve.wait_ge(conv_ready, h + 1)
                    dve.wait_ge(resid_ready, image_at(it, k - 11) + 1)
                    half = resid[ring][:, part * BANK:(part + 1) * BANK]
                    nc.vector.scalar_tensor_tensor(out=half, in0=ps_misc[:, :], scalar=INV, in1=half,
                                                   op0=ALU.mult, op1=ALU.add).then_inc(result_ready, 1)
                h = half_at(it, k - 7)
                if j % HALF_TILES == 3 and exists(h, HALVES):
                    at = (k - 7) % STEPS
                    cols = slice(at, at + HALF_TILES)
                    ring = (k - 7) // MT % 2
                    dve.wait_ge(probs_ready, HALF_TILES * h + HALF_TILES)
                    nc.vector.reciprocal(inv_sum[:, cols], row_sum[:, cols]).then_inc(inv_sum_ready, 1)
                    dve.wait_ge(inv_sum_ready, h + 1)
                    nc.vector.tensor_scalar(out=row_scale[:, cols], in0=inv_sum[:, cols],
                                            scalar1=g_unit[:, ring:ring + 1], scalar2=1.0 / PROB_SCALE,
                                            op0=ALU.mult, op1=ALU.mult).then_inc(row_scale_ready, 1)
                if j == 7 and exists(image + 1, B):
                    peak_of_g(image + 1, (k // MT + 1) % 2)
                if j == 0 and exists(image, B):
                    r = k // MT % 2
                    dve.wait_ge(g_peak_everywhere, image + 1)
                    nc.vector.tensor_scalar(out=g_unit[:, r:r + 1], in0=g_peak_all[:, r:r + 1],
                                            scalar1=G_LEAST, scalar2=1.0 / G_TOP,
                                            op0=ALU.max, op1=ALU.mult).then_inc(g_unit_ready, 1)
                    dve.wait_ge(g_unit_ready, image + 1)
                    nc.vector.reciprocal(g_factor[:, r:r + 1], g_unit[:, r:r + 1]).then_inc(g_factor_ready, 1)
                t = tile_at(it, k - 2)
                if exists(t, TILES):
                    slot, ring = (k - 2) % HALF_TILES, (k - 2) // HALF_TILES % 2
                    for c in range(2):
                        where = (slice(None), slice(c * HALF_TILES, (c + 1) * HALF_TILES),
                                 slice(slot * P, (slot + 1) * P))
                        dve.wait_ge(pt_hi_ready, 2 * t + c + 1)
                        nc.vector.scalar_tensor_tensor(
                            out=pt_lo[ring][where], in0=ps_flip[c][:, :].rearrange("p (a n) -> p a n", n=P),
                            scalar=PROB_SCALE, in1=pt_hi[ring][where],
                            op0=ALU.mult, op1=ALU.subtract).then_inc(pt_lo_ready, 1)
                t = tile_at(it, k + 1)
                if exists(t, TILES):
                    row_maximum(t, k + 1)

            run_steps(dve, step)

        @block.tensor
        def _(pe):
            def project(b, c, r, arrived, target):
                pe.wait_ge(x_arrived[r], arrived)
                nc.tensor.matmul(target[:, :], wqk[:, :], x_in[r][:, c * BANK:(c + 1) * BANK],
                                 start=True, stop=True).then_inc(proj_ready, 1)

            def project_g(r, target):
                for m in range(MT):
                    last = nc.tensor.matmul(target[:, m * CI:(m + 1) * CI], x_in[r][:, m * P:(m + 1) * P],
                                            wg[:, :], start=True, stop=True)
                last.then_inc(g_ready, 1)

            def scores(t, it, k):
                r, cols = k // MT % 2, slice(k % MT * P, (k % MT + 1) * P)
                if k % MT == 0:
                    turns = image_at(it, k) // 2 + 1 if isinstance(t, int) else it + (k // STEPS + 1)
                    pe.wait_ge(lo_ready, image_at(it, k) + 1)
                    pe.wait_ge(swapped[r], turns * 64)
                wait(pe, probs_ready, t - 1)
                top, low = slice(0, CI), slice(CI, P)
                terms = [(hi[r], hi_sw[r], hi_sw[r], hi[r]), (lo[r], hi_sw[r], lo_sw[r], hi[r]),
                         (hi[r], lo_sw[r], hi_sw[r], lo[r])]
                for n, (theta0, phi0, theta1, phi1) in enumerate(terms):
                    flags = dict(start=(n == 0), stop=(n == len(terms) - 1))
                    nc.tensor.matmul(ps_scores[k % 2][:, 0:BANK], theta0[top, cols], phi0[top, 0:BANK], **flags)
                    last = nc.tensor.matmul(ps_scores[k % 2][:, BANK:N], theta1[low, cols], phi1[low, BANK:N],
                                            **flags)
                last.then_inc(scores_ready, 1)

            pe.wait_ge(weights_in, 80)
            project(0, 0, 0, 16, ps_misc)
            project(0, 1, 0, 16, ps_y)
            project_g(0, ps_flip[0])
            nc.tensor.matmul(ps_flip[1][:, 0:1], wout[0:CI, 0:C], wout[0:CI, C:C + 1],
                             start=True, stop=True).then_inc(g_bias_ready, 1)
            scores(0, 0, 0)
            pe.wait_ge(ident_ready, 1)

            def step(it, k):
                image, j = image_at(it, k), k % MT
                t = tile_at(it, k + 1)
                if exists(t, TILES):
                    scores(t, it, k + 1)

                h, quarter = half_at(it, k - 6), (k - 6) % HALF_TILES
                if exists(h, HALVES):
                    ring, g = (k - 6) // HALF_TILES % 2, g_parts[(k - 6) // MT % 2]
                    if quarter == 0:
                        pe.wait_ge(pt_lo_ready, 2 * HALF_TILES * h + 2 * HALF_TILES)
                        pe.wait_ge(g_split, image_at(it, k - 6) + 1)
                        wait(pe, y_scaled, h)
                        wait(pe, proj_out, 2)
                    for m in (2 * quarter, 2 * quarter + 1):
                        nc.tensor.matmul(ps_y[:, :], g[:, m, :], pt_hi[ring][:, m, :],
                                         start=(m == 0), stop=False, skip_group_check=True)
                    for side in range(2):
                        m = 2 * quarter + side
                        last = nc.tensor.matmul(ps_y[side * CI:(side + 1) * CI, :], g[:, m, 0:CI],
                                                pt_lo[ring][:, m, :], start=False, stop=(m >= MT - 2),
                                                skip_group_check=True)
                    if quarter == HALF_TILES - 1:
                        last.then_inc(y_ready, 1)

                t = tile_at(it, k - 1)
                if exists(t, TILES):
                    pe.wait_ge(probs_ready, t + 1)
                    for c in range(2):
                        if isinstance(t, int) and t == 0:
                            pe.wait_ge(*((g_out, 1), (shift_ready, 1))[c])
                        wait(pe, pt_lo_ready, 2 * t + c - 1)
                        for a in range(HALF_TILES):
                            m = c * HALF_TILES + a
                            last = nc.tensor.transpose(ps_flip[c][:, a * P:(a + 1) * P],
                                                       probs[(k - 1) % 2][:, m * P:(m + 1) * P], ident[:, :])
                        last.then_inc(flipped, 1)

                more = exists(image + 1, B)
                if j % HALF_TILES == 0:
                    h = half_at(it, k - 8)
                    if exists(h, HALVES):
                        at = (k - 8) % STEPS
                        pe.wait_ge(row_scale_ready, h + 1)
                        wait(pe, result_ready, h)
                        if more and j == 4:
                            pe.wait_ge(proj_out, 2 * image + 4)
                        for a in range(HALF_TILES):
                            last = nc.tensor.transpose(
                                ps_misc[:, a * P:(a + 1) * P],
                                row_scale[:, at + a:at + a + 1].broadcast_to([P, P]), ident[:, :])
                        last.then_inc(spread_ready, 1)
                if j % HALF_TILES == 2:
                    h = half_at(it, k - 10)
                    if exists(h, HALVES):
                        pe.wait_ge(y_scaled, h + 1)
                        if more and j == 2:
                            pe.wait_ge(proj_out, 2 * image + 3)
                        if more and j == 6:
                            pe.wait_ge(g_out, image + 2)
                        nc.tensor.matmul(ps_misc[:, :], wout[:, 0:C], y_norm[:, :],
                                         start=True, stop=True).then_inc(conv_ready, 1)
                if j in (1, 3, 5) and more:
                    r = (k // MT + 1) % 2
                    arrived = 16 * ((image + 1) // 2 + 1) if isinstance(image, int) else \
                        it * 16 + 16 * ((k // MT + 1) // 2 + 1)
                    if j == 1:
                        wait(pe, spread_out, 2 * image - 1)
                        project(image + 1, 0, r, arrived, ps_misc)
                    if j == 3:
                        wait(pe, result_ready, 2 * image - 1)
                        wait(pe, proj_out, 2 * image + 3)
                        project(image + 1, 1, r, arrived, ps_misc)
                    if j == 5:
                        wait(pe, spread_out, 2 * image)
                        wait(pe, proj_out, 2 * image + 4)
                        project_g(r, ps_misc)

            run_steps(pe, step)


def kernel(x, L0_conv_w_g, L0_conv_b_g, L0_conv_w_theta, L0_conv_b_theta, L0_conv_w_phi, L0_conv_b_phi,
           L0_conv_w_out, L0_conv_b_out, L0_conv_bn_gamma, L0_conv_bn_beta, L0_conv_bn_mean, L0_conv_bn_var):
    import concourse.bacc as bacc
    import numpy as np
    from concourse import mybir
    from concourse.bass_utils import run_bass_kernel_spmd

    def rows(*parts):
        return np.ascontiguousarray(np.stack([np.asarray(p) for p in parts], axis=1))

    w_qk_t = np.ascontiguousarray(np.concatenate([L0_conv_w_theta, L0_conv_w_phi]).T)
    w_g_t = np.ascontiguousarray(np.asarray(L0_conv_w_g).T)
    w_out_t = np.ascontiguousarray(np.concatenate([np.asarray(L0_conv_w_out).T,
                                                   np.asarray(L0_conv_b_g)[:, None]], axis=1))
    vectors = rows(np.concatenate([L0_conv_b_theta, L0_conv_b_phi]), L0_conv_b_out, L0_conv_bn_gamma,
                   L0_conv_bn_beta, L0_conv_bn_mean, L0_conv_bn_var)
    arrays = {"x_in_dram": np.ascontiguousarray(x), "w_qk_t_dram": w_qk_t, "w_g_t_dram": w_g_t,
              "w_out_t_dram": w_out_t, "vectors_dram": vectors}
    nc = bacc.Bacc("TRN2", target_bir_lowering=False, num_devices=1)
    args = [nc.dram_tensor(name, a.shape, mybir.dt.from_np(a.dtype), kind="ExternalInput").ap()
            for name, a in arrays.items()]
    shape = arrays["x_in_dram"].shape
    out = nc.dram_tensor("out_dram", shape, mybir.dt.float32, kind="ExternalOutput").ap()
    build_nonlocal_attention(nc, *args, out)
    return run_bass_kernel_spmd(nc, [arrays], core_ids=[0]).results[0]["out_dram"]
```

```python
def build_nonlocal_attention(nc, x, w_qk_t, w_g_t, w_out_t, channel_vectors, out):
    from contextlib import ExitStack

    import concourse.bass as bass
    from concourse import mybir

    F32 = mybir.dt.float32
    F32R = mybir.dt.float32r
    F16 = mybir.dt.float16
    ALU = mybir.AluOpType
    ACT = mybir.ActivationFunctionType
    AX = mybir.AxisListType

    B, C, H, W = x.shape
    N = H * W
    CI = w_g_t.shape[1]
    P = 128
    BANK = 512
    EPS = 1e-5
    PROB_SCALE = 2.0 ** 15
    G_TOP = 2.0 ** 14
    G_LEAST = 1e-30

    MT = N // P
    TILES = B * MT
    HALF_TILES = BANK // P
    HALVES = TILES // HALF_TILES
    PER_IMAGE = N // BANK
    STEPS = 2 * MT
    LAG = 7
    STACKS = 6
    assert (C, CI, MT, PER_IMAGE, HALF_TILES) == (P, P // 2, 8, 2, 4) and B % 2 == 0

    x_v = x.rearrange("b c h w -> c b (h w)")
    out_v = out.rearrange("b c h w -> c b (h w)")

    with ExitStack() as ctx:
        def sbuf(name, shape, dt):
            return ctx.enter_context(nc.sbuf_tensor(name, shape, dt))

        def psum(name, shape, dt=F32):
            return ctx.enter_context(nc.psum_tensor(name, shape, dt))

        def sem(name):
            return ctx.enter_context(nc.semaphore(name))

        wqk = sbuf("wqk", [P, P], F32)
        wg = sbuf("wg", [P, CI], F32)
        wout = sbuf("wout", [P, C + 1], F32)
        vec = sbuf("vec", [P, 6], F32)
        ident = sbuf("ident", [P, P], F32)
        bn = sbuf("bn", [P, 8], F32)
        BIAS_QK, B_OUT, GAMMA, BETA, MEAN, VAR = (vec[:, i:i + 1] for i in range(6))
        VAR_EPS, STD, RSTD, INV, MEAN_INV, BETA_SHIFT, BIAS_SUM, SHIFT = (bn[:, i:i + 1] for i in range(8))

        x_in = [sbuf(f"x_in{i}", [P, N], F32) for i in range(2)]
        qk = sbuf("qk", [P, N], F32)
        hi = sbuf("hi", [P, N], F32R)
        lo = sbuf("lo", [P, N], F32R)
        theta_hl = [sbuf(f"theta_hl{i}", [P, N], F32R) for i in range(2)]
        phi_hh = [sbuf(f"phi_hh{i}", [P, N], F32R) for i in range(2)]
        phi_ll = [sbuf(f"phi_ll{i}", [P, N], F32R) for i in range(2)]
        g_raw = sbuf("g_raw", [P, MT, CI], F32)
        g_scaled = sbuf("g_scaled", [P, MT, CI], F32)
        g_parts = [sbuf(f"g_parts{i}", [P, MT, 2 * CI], F16) for i in range(2)]
        g_peak = sbuf("g_peak", [P, 2], F32)
        g_peak_all = sbuf("g_peak_all", [P, 2], F32)
        g_unit = sbuf("g_unit", [P, 2], F32)
        g_factor = sbuf("g_factor", [P, 2], F32)
        resid = [sbuf(f"resid{i}", [P, N], F32) for i in range(2)]

        probs = [sbuf(f"probs{i}", [P, N], F32) for i in range(2)]
        neg_max = sbuf("neg_max", [P, STEPS], F32)
        row_sum = sbuf("row_sum", [P, STEPS], F32)
        inv_sum = sbuf("inv_sum", [P, STEPS], F32)
        row_scale = sbuf("row_scale", [P, STEPS], F32)
        pt_hi = [sbuf(f"pt_hi{i}", [P, MT, BANK], F16) for i in range(2)]
        pt_lo = [sbuf(f"pt_lo{i}", [P, MT, BANK], F16) for i in range(2)]
        scale_row = sbuf("scale_row", [P, BANK], F32)
        y_norm = sbuf("y_norm", [P, BANK], F32)

        ps_scores = [psum(f"ps_scores{i}", [P, N]) for i in range(2)]
        ps_flip = [psum(f"ps_flip{i}", [P, BANK]) for i in range(2)]
        ps_y = psum("ps_y", [P, BANK])
        ps_misc = psum("ps_misc", [P, BANK])

        weights_in = sem("weights_in")
        x_arrived = [sem(f"x_arrived{i}") for i in range(2)]
        stacked = [sem(f"stacked{i}") for i in range(2)]
        stored = [sem(f"stored{i}") for i in range(2)]
        ident_zero = sem("ident_zero")
        ident_ready = sem("ident_ready")
        bn_step = sem("bn_step")
        bn_std = sem("bn_std")
        g_bias_ready = sem("g_bias_ready")
        shift_ready = sem("shift_ready")
        proj_ready = sem("proj_ready")
        proj_out = sem("proj_out")
        hi_ready = sem("hi_ready")
        lo_ready = sem("lo_ready")
        g_ready = sem("g_ready")
        g_out = sem("g_out")
        g_peak_ready = sem("g_peak_ready")
        g_peak_everywhere = sem("g_peak_everywhere")
        g_unit_ready = sem("g_unit_ready")
        g_factor_ready = sem("g_factor_ready")
        g_hi_ready = sem("g_hi_ready")
        g_scaled_ready = sem("g_scaled_ready")
        g_split = sem("g_split")
        resid_ready = sem("resid_ready")
        scores_ready = sem("scores_ready")
        max_ready = sem("max_ready")
        probs_ready = sem("probs_ready")
        flipped = sem("flipped")
        pt_hi_ready = sem("pt_hi_ready")
        pt_lo_ready = sem("pt_lo_ready")
        y_ready = sem("y_ready")
        inv_sum_ready = sem("inv_sum_ready")
        row_scale_ready = sem("row_scale_ready")
        spread_ready = sem("spread_ready")
        spread_out = sem("spread_out")
        y_scaled = sem("y_scaled")
        conv_ready = sem("conv_ready")
        result_ready = sem("result_ready")

        block = ctx.enter_context(nc.Block())

        def tile_at(it, k):
            return it * STEPS + k

        def half_at(it, k):
            return it * (STEPS // HALF_TILES) + k // HALF_TILES

        def image_at(it, k):
            return it * (STEPS // MT) + k // MT

        def exists(index, count):
            return not isinstance(index, int) or 0 <= index < count

        def wait(eng, semaphore, value):
            if not isinstance(value, int) or value > 0:
                eng.wait_ge(semaphore, value)

        def run_steps(eng, step):
            for k in range(MT):
                step(0, k)
            with eng.Fori(0, B // 2 - 1) as it:
                for k in range(MT, MT + STEPS):
                    step(it, k)
            for k in range(MT, STEPS + LAG):
                step(B // 2 - 1, k)

        @block.sync
        def _(sp):
            sp.dma_start(x_in[0][:, :], x_v[:, 0, :]).then_inc(x_arrived[0], 16)
            sp.dma_start(wqk[:, :], w_qk_t).then_inc(weights_in, 16)
            sp.dma_start(wg[:, :], w_g_t).then_inc(weights_in, 16)
            sp.dma_start(wout[0:CI, :], w_out_t).then_inc(weights_in, 16)
            sp.dma_start(wout[CI:P, :], w_out_t).then_inc(weights_in, 16)
            sp.dma_start(vec[:, :], channel_vectors).then_inc(weights_in, 16)
            sp.dma_start(x_in[1][:, :], x_v[:, 1, :]).then_inc(x_arrived[1], 16)

            def store(it, k):
                h = half_at(it, k)
                if not exists(h, HALVES):
                    return
                part = (k // HALF_TILES) % PER_IMAGE
                ring = (k // MT) % 2
                sp.wait_ge(result_ready, h + 1)
                cols = slice(part * BANK, (part + 1) * BANK)
                dst = out_v[:, image_at(it, k), cols] if isinstance(h, int) else \
                    out_v[:, bass.ds(image_at(it, k), 1), cols]
                sp.dma_start(dst, resid[ring][:, cols]).then_inc(stored[ring], 16)

            def restack(target, to, source, start, r):
                sp.dma_start(target[to:to + CI, :].bitcast(F32),
                             source[start:start + CI, :].bitcast(F32)).then_inc(stacked[r], 16)

            def image(it, k):
                b, r = image_at(it, k), (k // MT) % 2
                store(it, k - 2 * MT)
                sp.wait_ge(hi_ready, b + 1)
                restack(theta_hl[r], 0, hi, 0, r)
                restack(phi_hh[r], 0, hi, CI, r)
                restack(phi_hh[r], CI, hi, CI, r)
                sp.wait_ge(lo_ready, b + 1)
                restack(theta_hl[r], CI, lo, 0, r)
                restack(phi_ll[r], 0, lo, CI, r)
                restack(phi_ll[r], CI, lo, CI, r)
                store(it, k - 2 * MT + HALF_TILES)
                if exists(b + 2, B):
                    sp.wait_ge(proj_ready, 2 * b + 2)
                    sp.wait_ge(g_ready, b + 1)
                    sp.wait_ge(resid_ready, b + 1)
                    src = x_v[:, b + 2, :] if isinstance(b, int) else x_v[:, bass.ds(b + 2, 1), :]
                    sp.dma_start(x_in[r][:, :], src).then_inc(x_arrived[r], 16)

            image(0, 0)
            image(0, MT)
            with sp.Fori(1, B // 2 - 1) as it:
                image(it, 0)
                image(it, MT)
            image(B // 2 - 1, 0)
            image(B // 2 - 1, MT)
            for k in range(0, STEPS, HALF_TILES):
                store(B // 2 - 1, k)
            for r in range(2):
                sp.wait_ge(stored[r], 16 * HALVES // 2)

        @block.gpsimd
        def _(pool):
            nc.gpsimd.memset(ident[:, :], 0.0).then_inc(ident_zero, 1)
            pool.wait_ge(ident_zero, 1)
            nc.gpsimd.affine_select(out=ident[:, :], in_=ident[:, :], compare_op=ALU.not_equal, fill=1.0,
                                    base=0, pattern=[[-1, P]], channel_multiplier=1).then_inc(ident_ready, 1)

            def image(b):
                r = b % 2
                pool.wait_ge(proj_out, 2 * b + 2)
                wait(pool, scores_ready, (b - 1) * MT)
                if b >= 1:
                    pool.wait_ge(stacked[1 - r], 16 * STACKS * ((b + 1) // 2))
                nc.gpsimd.tensor_scalar(out=hi[:, :], in0=qk[:, :], scalar1=1.0, scalar2=0.0,
                                        op0=ALU.mult, op1=ALU.add).then_inc(hi_ready, 1)
                pool.wait_ge(hi_ready, b + 1)
                nc.gpsimd.tensor_tensor(lo[:, :], qk[:, :], hi[:, :].bitcast(F32),
                                        ALU.subtract).then_inc(lo_ready, 1)
                pool.wait_ge(g_peak_ready, b + 1)
                nc.gpsimd.partition_all_reduce(g_peak_all[:, r:r + 1], g_peak[:, r:r + 1], P,
                                               bass.bass_isa.ReduceOp.max).then_inc(g_peak_everywhere, 1)
                pool.wait_ge(g_factor_ready, b + 1)
                wait(pool, y_ready, (b - 1) * PER_IMAGE)
                nc.gpsimd.tensor_scalar(out=g_parts[r][:, :, 0:CI], in0=g_raw[:, :, :],
                                        scalar1=g_factor[:, r:r + 1], scalar2=1.0,
                                        op0=ALU.mult, op1=ALU.mult).then_inc(g_hi_ready, 1)
                nc.gpsimd.tensor_scalar(out=g_scaled[:, :, :], in0=g_raw[:, :, :],
                                        scalar1=g_factor[:, r:r + 1], scalar2=1.0,
                                        op0=ALU.mult, op1=ALU.mult).then_inc(g_scaled_ready, 1)
                pool.wait_ge(g_hi_ready, b + 1)
                pool.wait_ge(g_scaled_ready, b + 1)
                nc.gpsimd.tensor_tensor(g_parts[r][:, :, CI:2 * CI], g_scaled[:, :, :],
                                        g_parts[r][:, :, 0:CI], ALU.subtract).then_inc(g_split, 1)
                pool.wait_ge(shift_ready, 1)
                pool.wait_ge(x_arrived[r], 16 * (b // 2 + 1))
                wait(pool, stored[r], 16 * PER_IMAGE * (b // 2))
                nc.gpsimd.tensor_scalar(out=resid[r][:, :], in0=x_in[r][:, :], scalar1=SHIFT, scalar2=1.0,
                                        op0=ALU.add, op1=ALU.mult).then_inc(resid_ready, 1)

            for b in range(B):
                image(b)

        @block.scalar
        def _(act):
            def evacuate_projection(b, c, source):
                act.wait_ge(proj_ready, 2 * b + c + 1)
                wait(act, lo_ready, b)
                nc.scalar.activation(qk[:, c * BANK:(c + 1) * BANK], source[:, :], ACT.Identity,
                                     bias=BIAS_QK).then_inc(proj_out, 1)

            def evacuate_g(b, source):
                act.wait_ge(g_ready, b + 1)
                wait(act, g_split, b)
                nc.scalar.activation(g_raw[:, :, :].rearrange("p t c -> p (t c)"), source[:, :],
                                     ACT.Copy).then_inc(g_out, 1)

            act.wait_ge(bn_step, 1)
            nc.scalar.activation(STD, VAR_EPS, ACT.Sqrt).then_inc(bn_std, 1)
            act.wait_ge(weights_in, 80)
            evacuate_projection(0, 0, ps_misc)
            evacuate_projection(0, 1, ps_y)
            evacuate_g(0, ps_flip[0])

            def step(it, k):
                image, j = image_at(it, k), k % MT
                h = half_at(it, k - 8)
                if j % HALF_TILES == 0 and exists(h, HALVES):
                    act.wait_ge(spread_ready, h + 1)
                    wait(act, y_scaled, h)
                    nc.scalar.activation(scale_row[:, :], ps_misc[:, :], ACT.Copy).then_inc(spread_out, 1)
                if j in (1, 3) and exists(image + 1, B):
                    evacuate_projection(image + 1, j // 2, ps_misc)
                if j == 5 and exists(image + 1, B):
                    evacuate_g(image + 1, ps_misc)
                t = tile_at(it, k - 1)
                if exists(t, TILES):
                    slot, ring = (k - 1) % HALF_TILES, (k - 1) // HALF_TILES % 2
                    if slot == 0:
                        wait(act, y_ready, half_at(it, k - 1) - 1)
                    for c in range(2):
                        act.wait_ge(flipped, 2 * t + c + 1)
                        nc.scalar.activation(
                            pt_hi[ring][:, c * HALF_TILES:(c + 1) * HALF_TILES, slot * P:(slot + 1) * P],
                            ps_flip[c][:, :].rearrange("p (a n) -> p a n", n=P),
                            ACT.Copy, scale=PROB_SCALE).then_inc(pt_hi_ready, 1)
                t = tile_at(it, k)
                if exists(t, TILES):
                    act.wait_ge(max_ready, t + 1)
                    wait(act, flipped, 2 * t - 2)
                    nc.scalar.activation(probs[k % 2][:, :], ps_scores[k % 2][:, :], ACT.Exp,
                                         bias=neg_max[:, k % STEPS:k % STEPS + 1],
                                         accum_out=row_sum[:, k % STEPS:k % STEPS + 1]).then_inc(probs_ready, 1)

            run_steps(act, step)

        @block.vector
        def _(dve):
            dve.wait_ge(weights_in, 80)
            nc.vector.tensor_scalar(out=VAR_EPS, in0=VAR, scalar1=EPS, scalar2=None,
                                    op0=ALU.add).then_inc(bn_step, 1)
            dve.wait_ge(bn_std, 1)
            nc.vector.reciprocal(RSTD, STD).then_inc(bn_step, 1)
            dve.wait_ge(bn_step, 2)
            nc.vector.tensor_tensor(INV, GAMMA, RSTD, ALU.mult).then_inc(bn_step, 1)
            dve.wait_ge(bn_step, 3)
            nc.vector.tensor_tensor(MEAN_INV, MEAN, INV, ALU.mult).then_inc(bn_step, 1)
            dve.wait_ge(bn_step, 4)
            nc.vector.tensor_tensor(BETA_SHIFT, BETA, MEAN_INV, ALU.subtract).then_inc(bn_step, 1)

            def peak_of_g(b, r):
                dve.wait_ge(g_out, b + 1)
                nc.vector.tensor_reduce(out=g_peak[:, r:r + 1], in_=g_raw[:, :, :], op=ALU.max, axis=AX.XY,
                                        apply_absolute_value=True).then_inc(g_peak_ready, 1)

            def row_maximum(t, k):
                dve.wait_ge(scores_ready, t + 1)
                nc.vector.tensor_reduce(out=neg_max[:, k % STEPS:k % STEPS + 1], in_=ps_scores[k % 2][:, :],
                                        op=ALU.max, axis=AX.X, negate=True).then_inc(max_ready, 1)

            peak_of_g(0, 0)
            dve.wait_ge(g_bias_ready, 1)
            nc.vector.tensor_tensor(BIAS_SUM, ps_flip[1][:, 0:1], B_OUT, ALU.add).then_inc(bn_step, 1)
            dve.wait_ge(bn_step, 6)
            nc.vector.scalar_tensor_tensor(out=SHIFT, in0=BIAS_SUM, scalar=INV, in1=BETA_SHIFT,
                                           op0=ALU.mult, op1=ALU.add).then_inc(shift_ready, 1)
            row_maximum(0, 0)

            def step(it, k):
                image, j = image_at(it, k), k % MT
                h = half_at(it, k - 9)
                if j % HALF_TILES == 1 and exists(h, HALVES):
                    dve.wait_ge(y_ready, h + 1)
                    dve.wait_ge(spread_out, h + 1)
                    wait(dve, conv_ready, h)
                    nc.vector.tensor_tensor(y_norm[:, :], ps_y[:, :], scale_row[:, :],
                                            ALU.mult).then_inc(y_scaled, 1)
                h = half_at(it, k - 10)
                if j % HALF_TILES == 2 and exists(h, HALVES):
                    ring, part = (k - 10) // MT % 2, (k - 10) // HALF_TILES % PER_IMAGE
                    dve.wait_ge(conv_ready, h + 1)
                    dve.wait_ge(resid_ready, image_at(it, k - 10) + 1)
                    half = resid[ring][:, part * BANK:(part + 1) * BANK]
                    nc.vector.scalar_tensor_tensor(out=half, in0=ps_misc[:, :], scalar=INV, in1=half,
                                                   op0=ALU.mult, op1=ALU.add).then_inc(result_ready, 1)
                h = half_at(it, k - 6)
                if j % HALF_TILES == 2 and exists(h, HALVES):
                    at = (k - 6) % STEPS
                    cols = slice(at, at + HALF_TILES)
                    ring = (k - 6) // MT % 2
                    dve.wait_ge(probs_ready, HALF_TILES * h + HALF_TILES)
                    nc.vector.reciprocal(inv_sum[:, cols], row_sum[:, cols]).then_inc(inv_sum_ready, 1)
                    dve.wait_ge(inv_sum_ready, h + 1)
                    nc.vector.tensor_scalar(out=row_scale[:, cols], in0=inv_sum[:, cols],
                                            scalar1=g_unit[:, ring:ring + 1], scalar2=1.0 / PROB_SCALE,
                                            op0=ALU.mult, op1=ALU.mult).then_inc(row_scale_ready, 1)
                if j == 6 and exists(image + 1, B):
                    peak_of_g(image + 1, (k // MT + 1) % 2)
                if j == 0 and exists(image, B):
                    r = k // MT % 2
                    dve.wait_ge(g_peak_everywhere, image + 1)
                    nc.vector.tensor_scalar(out=g_unit[:, r:r + 1], in0=g_peak_all[:, r:r + 1],
                                            scalar1=G_LEAST, scalar2=1.0 / G_TOP,
                                            op0=ALU.max, op1=ALU.mult).then_inc(g_unit_ready, 1)
                    dve.wait_ge(g_unit_ready, image + 1)
                    nc.vector.reciprocal(g_factor[:, r:r + 1], g_unit[:, r:r + 1]).then_inc(g_factor_ready, 1)
                t = tile_at(it, k - 1)
                if exists(t, TILES):
                    slot, ring = (k - 1) % HALF_TILES, (k - 1) // HALF_TILES % 2
                    for c in range(2):
                        where = (slice(None), slice(c * HALF_TILES, (c + 1) * HALF_TILES),
                                 slice(slot * P, (slot + 1) * P))
                        dve.wait_ge(pt_hi_ready, 2 * t + c + 1)
                        nc.vector.scalar_tensor_tensor(
                            out=pt_lo[ring][where], in0=ps_flip[c][:, :].rearrange("p (a n) -> p a n", n=P),
                            scalar=PROB_SCALE, in1=pt_hi[ring][where],
                            op0=ALU.mult, op1=ALU.subtract).then_inc(pt_lo_ready, 1)
                t = tile_at(it, k + 1)
                if exists(t, TILES):
                    row_maximum(t, k + 1)

            run_steps(dve, step)

        @block.tensor
        def _(pe):
            def project(b, c, r, arrived, target):
                pe.wait_ge(x_arrived[r], arrived)
                nc.tensor.matmul(target[:, :], wqk[:, :], x_in[r][:, c * BANK:(c + 1) * BANK],
                                 start=True, stop=True).then_inc(proj_ready, 1)

            def project_g(r, target):
                for m in range(MT):
                    last = nc.tensor.matmul(target[:, m * CI:(m + 1) * CI], x_in[r][:, m * P:(m + 1) * P],
                                            wg[:, :], start=True, stop=True)
                last.then_inc(g_ready, 1)

            def scores(t, it, k):
                r, cols = k // MT % 2, slice(k % MT * P, (k % MT + 1) * P)
                if k % MT == 0:
                    turns = image_at(it, k) // 2 + 1 if isinstance(t, int) else it + (k // STEPS + 1)
                    pe.wait_ge(stacked[r], turns * 16 * STACKS)
                wait(pe, probs_ready, t - 1)
                for n, phi in enumerate((phi_hh[r], phi_ll[r])):
                    for c in range(PER_IMAGE):
                        cc = slice(c * BANK, (c + 1) * BANK)
                        last = nc.tensor.matmul(ps_scores[k % 2][:, cc], theta_hl[r][:, cols], phi[:, cc],
                                                start=(n == 0), stop=(n == 1))
                last.then_inc(scores_ready, 1)

            pe.wait_ge(weights_in, 80)
            project(0, 0, 0, 16, ps_misc)
            project(0, 1, 0, 16, ps_y)
            project_g(0, ps_flip[0])
            nc.tensor.matmul(ps_flip[1][:, 0:1], wout[0:CI, 0:C], wout[0:CI, C:C + 1],
                             start=True, stop=True).then_inc(g_bias_ready, 1)
            scores(0, 0, 0)
            pe.wait_ge(ident_ready, 1)

            def step(it, k):
                image, j = image_at(it, k), k % MT
                t = tile_at(it, k - 1)
                if exists(t, TILES):
                    pe.wait_ge(probs_ready, t + 1)
                    for c in range(2):
                        if isinstance(t, int) and t == 0:
                            pe.wait_ge(*((g_out, 1), (shift_ready, 1))[c])
                        wait(pe, pt_lo_ready, 2 * t + c - 1)
                        for a in range(HALF_TILES):
                            m = c * HALF_TILES + a
                            last = nc.tensor.transpose(ps_flip[c][:, a * P:(a + 1) * P],
                                                       probs[(k - 1) % 2][:, m * P:(m + 1) * P], ident[:, :])
                        last.then_inc(flipped, 1)

                t = tile_at(it, k + 1)
                if exists(t, TILES):
                    scores(t, it, k + 1)

                h, quarter = half_at(it, k - 5), (k - 5) % HALF_TILES
                if exists(h, HALVES):
                    ring, g = (k - 5) // HALF_TILES % 2, g_parts[(k - 5) // MT % 2]
                    if quarter == 0:
                        pe.wait_ge(pt_lo_ready, 2 * HALF_TILES * h + 2 * HALF_TILES)
                        pe.wait_ge(g_split, image_at(it, k - 5) + 1)
                        wait(pe, y_scaled, h)
                        wait(pe, proj_out, 2)
                    for m in (2 * quarter, 2 * quarter + 1):
                        nc.tensor.matmul(ps_y[:, :], g[:, m, :], pt_hi[ring][:, m, :],
                                         start=(m == 0), stop=False, skip_group_check=True)
                    for side in range(2):
                        m = 2 * quarter + side
                        last = nc.tensor.matmul(ps_y[side * CI:(side + 1) * CI, :], g[:, m, 0:CI],
                                                pt_lo[ring][:, m, :], start=False, stop=(m >= MT - 2),
                                                skip_group_check=True)
                    if quarter == HALF_TILES - 1:
                        last.then_inc(y_ready, 1)

                more = exists(image + 1, B)
                if j % HALF_TILES == 3:
                    h = half_at(it, k - 7)
                    if exists(h, HALVES):
                        at = (k - 7) % STEPS
                        pe.wait_ge(row_scale_ready, h + 1)
                        wait(pe, result_ready, h)
                        if more and j == 3:
                            pe.wait_ge(proj_out, 2 * image + 4)
                        for a in range(HALF_TILES):
                            last = nc.tensor.transpose(
                                ps_misc[:, a * P:(a + 1) * P],
                                row_scale[:, at + a:at + a + 1].broadcast_to([P, P]), ident[:, :])
                        last.then_inc(spread_ready, 1)
                if j % HALF_TILES == 1:
                    h = half_at(it, k - 9)
                    if exists(h, HALVES):
                        pe.wait_ge(y_scaled, h + 1)
                        if more and j == 1:
                            pe.wait_ge(proj_out, 2 * image + 3)
                        if more and j == 5:
                            pe.wait_ge(g_out, image + 2)
                        nc.tensor.matmul(ps_misc[:, :], wout[:, 0:C], y_norm[:, :],
                                         start=True, stop=True).then_inc(conv_ready, 1)
                if j in (0, 2, 4) and more:
                    r = (k // MT + 1) % 2
                    arrived = 16 * ((image + 1) // 2 + 1) if isinstance(image, int) else \
                        it * 16 + 16 * ((k // MT + 1) // 2 + 1)
                    if j == 0:
                        wait(pe, spread_out, 2 * image - 1)
                        project(image + 1, 0, r, arrived, ps_misc)
                    if j == 2:
                        wait(pe, result_ready, 2 * image - 1)
                        wait(pe, proj_out, 2 * image + 3)
                        project(image + 1, 1, r, arrived, ps_misc)
                    if j == 4:
                        wait(pe, spread_out, 2 * image)
                        wait(pe, proj_out, 2 * image + 4)
                        project_g(r, ps_misc)

            run_steps(pe, step)


def kernel(x, L0_conv_w_g, L0_conv_b_g, L0_conv_w_theta, L0_conv_b_theta, L0_conv_w_phi, L0_conv_b_phi,
           L0_conv_w_out, L0_conv_b_out, L0_conv_bn_gamma, L0_conv_bn_beta, L0_conv_bn_mean, L0_conv_bn_var):
    import concourse.bacc as bacc
    import numpy as np
    from concourse import mybir
    from concourse.bass_utils import run_bass_kernel_spmd

    def rows(*parts):
        return np.ascontiguousarray(np.stack([np.asarray(p) for p in parts], axis=1))

    w_qk_t = np.ascontiguousarray(np.concatenate([L0_conv_w_theta, L0_conv_w_phi]).T)
    w_g_t = np.ascontiguousarray(np.asarray(L0_conv_w_g).T)
    w_out_t = np.ascontiguousarray(np.concatenate([np.asarray(L0_conv_w_out).T,
                                                   np.asarray(L0_conv_b_g)[:, None]], axis=1))
    vectors = rows(np.concatenate([L0_conv_b_theta, L0_conv_b_phi]), L0_conv_b_out, L0_conv_bn_gamma,
                   L0_conv_bn_beta, L0_conv_bn_mean, L0_conv_bn_var)
    arrays = {"x_in_dram": np.ascontiguousarray(x), "w_qk_t_dram": w_qk_t, "w_g_t_dram": w_g_t,
              "w_out_t_dram": w_out_t, "vectors_dram": vectors}
    nc = bacc.Bacc("TRN2", target_bir_lowering=False, num_devices=1)
    args = [nc.dram_tensor(name, a.shape, mybir.dt.from_np(a.dtype), kind="ExternalInput").ap()
            for name, a in arrays.items()]
    shape = arrays["x_in_dram"].shape
    out = nc.dram_tensor("out_dram", shape, mybir.dt.float32, kind="ExternalOutput").ap()
    build_nonlocal_attention(nc, *args, out)
    return run_bass_kernel_spmd(nc, [arrays], core_ids=[0]).results[0]["out_dram"]
```

```python
def build_nonlocal_attention(nc, x, w_tp_t, w_g_t, w_out_t, channel_vectors, out):
    from contextlib import ExitStack

    import concourse.bass as bass
    from concourse import mybir

    F32 = mybir.dt.float32
    F32R = mybir.dt.float32r
    F16 = mybir.dt.float16
    ALU = mybir.AluOpType
    ACT = mybir.ActivationFunctionType
    AX = mybir.AxisListType

    B, C, H, W = x.shape
    N = H * W
    CI = w_g_t.shape[1]
    P = 128
    BANK = 512
    EPS = 1e-5
    PROB_SCALE = 2.0 ** 15
    G_TOP = 2.0 ** 14
    G_LEAST = 1e-30

    MT = N // P
    TILES = B * MT
    HALF_TILES = BANK // P
    HALVES = TILES // HALF_TILES
    PER_IMAGE = N // BANK
    STEPS = 2 * MT
    LAG = 4
    STACKS = 6
    PROB_RING = 4
    WARM_UP = 6
    LAST_PIECES = (slice(0, BANK - P), slice(BANK - P, BANK))
    NEEDED_BY_TILE_0 = 3
    assert (C, CI, MT, PER_IMAGE, HALF_TILES) == (P, P // 2, 8, 2, 4) and B % 2 == 0

    x_v = x.rearrange("b c h w -> c b (h w)")
    out_v = out.rearrange("b c h w -> c b (h w)")

    with ExitStack() as ctx:
        def sbuf(name, shape, dt):
            return ctx.enter_context(nc.sbuf_tensor(name, shape, dt))

        def psum(name, shape, dt=F32):
            return ctx.enter_context(nc.psum_tensor(name, shape, dt))

        def sem(name):
            return ctx.enter_context(nc.semaphore(name))

        w_tp = sbuf("w_tp", [P, 4 * CI], F32)
        wg = sbuf("wg", [P, CI], F32)
        w_tp_hi = sbuf("w_tp_hi", [P, P], F32R)
        w_tp_lo = sbuf("w_tp_lo", [P, P], F32R)
        wout = sbuf("wout", [P, C + 1], F32)
        vec = sbuf("vec", [P, 8], F32)
        ident = sbuf("ident", [P, P], F32)
        warm = sbuf("warm", [P, P], F32)
        table_probe = sbuf("table_probe", [P, 1], F32)
        bn = sbuf("bn", [P, 8], F32)
        BIAS_TP, BIAS_TT, BIAS_PP, B_OUT, GAMMA, BETA, MEAN, VAR = (vec[:, i:i + 1] for i in range(8))
        VAR_EPS, STD, RSTD, INV, MEAN_INV, BETA_SHIFT, BIAS_SUM, SHIFT = (bn[:, i:i + 1] for i in range(8))

        x_in = [sbuf(f"x_in{i}", [P, N], F32) for i in range(2)]
        x_hi = sbuf("x_hi", [P, N], F32R)
        x_lo = sbuf("x_lo", [P, N], F32R)
        qk = sbuf("qk", [P, N], F32)
        hi = sbuf("hi", [P, N], F32R)
        lo = sbuf("lo", [P, N], F32R)
        theta_hl = [sbuf(f"theta_hl{i}", [P, N], F32R) for i in range(2)]
        phi_hh = [sbuf(f"phi_hh{i}", [P, N], F32R) for i in range(2)]
        phi_ll = [sbuf(f"phi_ll{i}", [P, N], F32R) for i in range(2)]
        g_channels = sbuf("g_channels", [P, BANK], F32)
        g_raw = sbuf("g_raw", [P, MT, CI], F32)
        g_scaled = sbuf("g_scaled", [P, MT, CI], F32)
        g_parts = [sbuf(f"g_parts{i}", [P, MT, 2 * CI], F16) for i in range(2)]
        g_peak = sbuf("g_peak", [P, 2], F32)
        g_peak_all = sbuf("g_peak_all", [P, 2], F32)
        g_unit = sbuf("g_unit", [P, 2], F32)
        g_factor = sbuf("g_factor", [P, 2], F32)
        y_unit = sbuf("y_unit", [P, 2], F32)
        resid = [sbuf(f"resid{i}", [P, N], F32) for i in range(2)]

        probs = [sbuf(f"probs{i}", [P, N], F32) for i in range(PROB_RING)]
        neg_max = sbuf("neg_max", [P, STEPS], F32)
        row_sum = sbuf("row_sum", [P, STEPS], F32)
        inv_sum = sbuf("inv_sum", [P, STEPS], F32)
        pt_hi = [sbuf(f"pt_hi{i}", [P, MT, BANK], F16) for i in range(2)]
        pt_lo = [sbuf(f"pt_lo{i}", [P, MT, BANK], F16) for i in range(2)]
        y_norm = sbuf("y_norm", [P, BANK], F32)

        ps_scores = [psum(f"ps_scores{i}", [P, N]) for i in range(2)]
        ps_flip = [psum(f"ps_flip{i}", [P, BANK]) for i in range(2)]
        ps_y = psum("ps_y", [P, BANK])
        ps_misc = psum("ps_misc", [P, BANK])

        first_order = ((0, slice(0, P), ps_misc[:, 0:P]), (1, slice(0, BANK), ps_scores[0][:, 0:BANK]),
                       (1, slice(BANK, N), ps_scores[0][:, BANK:N]),
                       (0, slice(P, BANK), ps_scores[1][:, P:BANK]),
                       (0, slice(BANK, N), ps_scores[1][:, BANK:N]))

        w_tp_in = sem("w_tp_in")
        w_g_in = sem("w_g_in")
        w_out_in = sem("w_out_in")
        vectors_in = sem("vectors_in")
        x_arrived = [[sem(f"x_arrived{i}{c}") for c in range(PER_IMAGE)] for i in range(2)]
        stacked = [sem(f"stacked{i}") for i in range(2)]
        stored = [sem(f"stored{i}") for i in range(2)]
        ident_zero = sem("ident_zero")
        ident_ready = sem("ident_ready")
        warm_ready = sem("warm_ready")
        bn_step = sem("bn_step")
        bn_std = sem("bn_std")
        g_bias_ready = sem("g_bias_ready")
        shift_ready = sem("shift_ready")
        first_proj = sem("first_proj")
        first_hi = sem("first_hi")
        first_lo = sem("first_lo")
        w_hi_ready = sem("w_hi_ready")
        w_lo_ready = sem("w_lo_ready")
        x_hi_ready = sem("x_hi_ready")
        x_lo_ready = sem("x_lo_ready")
        proj_ready = sem("proj_ready")
        proj_out = sem("proj_out")
        hi_ready = sem("hi_ready")
        lo_ready = sem("lo_ready")
        g_ready = sem("g_ready")
        g_channels_out = sem("g_channels_out")
        g_flipped = sem("g_flipped")
        g_out = sem("g_out")
        g_peak_ready = sem("g_peak_ready")
        g_peak_everywhere = sem("g_peak_everywhere")
        g_unit_ready = sem("g_unit_ready")
        g_factor_ready = sem("g_factor_ready")
        g_hi_ready = sem("g_hi_ready")
        g_scaled_ready = sem("g_scaled_ready")
        g_split = sem("g_split")
        resid_ready = sem("resid_ready")
        scores_ready = sem("scores_ready")
        max_ready = sem("max_ready")
        probs_ready = sem("probs_ready")
        flipped = sem("flipped")
        pt_hi_ready = sem("pt_hi_ready")
        pt_lo_ready = sem("pt_lo_ready")
        y_ready = sem("y_ready")
        inv_sum_ready = sem("inv_sum_ready")
        probs_scaled = sem("probs_scaled")
        y_unit_ready = sem("y_unit_ready")
        y_scaled = sem("y_scaled")
        conv_ready = sem("conv_ready")
        result_ready = sem("result_ready")

        block = ctx.enter_context(nc.Block())

        def tile_at(it, k):
            return it * STEPS + k

        def half_at(it, k):
            return it * (STEPS // HALF_TILES) + k // HALF_TILES

        def image_at(it, k):
            return it * (STEPS // MT) + k // MT

        def exists(index, count):
            return not isinstance(index, int) or 0 <= index < count

        def wait(eng, semaphore, value):
            if not isinstance(value, int) or value > 0:
                eng.wait_ge(semaphore, value)

        def tile_is(it, k, t):
            return isinstance(it, int) and tile_at(it, k) == t

        def is_first(image):
            return isinstance(image, int) and image == 0

        def run_steps(eng, step, head=MT):
            turns = (TILES - head - MT) // STEPS
            for k in range(head):
                step(0, k)
            with eng.Fori(0, turns) as it:
                for k in range(head, head + STEPS):
                    step(it, k)
            for k in range(head, TILES - turns * STEPS + LAG):
                step(turns, k)

        @block.sync
        def _(sp):
            def load_x(b, r):
                for c in range(PER_IMAGE):
                    cols = slice(c * BANK, (c + 1) * BANK)
                    src = x_v[:, b, cols] if isinstance(b, int) else x_v[:, bass.ds(b, 1), cols]
                    sp.dma_start(x_in[r][:, cols], src).then_inc(x_arrived[r][c], 16)

            load_x(0, 0)
            sp.dma_start(wg[:, :], w_g_t).then_inc(w_g_in, 16)
            sp.dma_start(wout[0:CI, :], w_out_t).then_inc(w_out_in, 16)
            sp.dma_start(wout[CI:P, :], w_out_t).then_inc(w_out_in, 16)
            load_x(1, 1)

            def store(it, k):
                h = half_at(it, k)
                if not exists(h, HALVES):
                    return
                part = (k // HALF_TILES) % PER_IMAGE
                ring = (k // MT) % 2
                sp.wait_ge(result_ready, h + 1)
                cols = slice(part * BANK, (part + 1) * BANK)
                dst = out_v[:, image_at(it, k), cols] if isinstance(h, int) else \
                    out_v[:, bass.ds(image_at(it, k), 1), cols]
                sp.dma_start(dst, resid[ring][:, cols]).then_inc(stored[ring], 16)

            def restack(target, to, source, start, r):
                sp.dma_start(target[to:to + CI, :].bitcast(F32),
                             source[start:start + CI, :].bitcast(F32)).then_inc(stacked[r], 16)

            def image(it, k):
                b, r = image_at(it, k), (k // MT) % 2
                store(it, k - 2 * MT + HALF_TILES)
                if exists(b + 2, B):
                    sp.wait_ge(g_ready, b + 1)
                    sp.wait_ge(resid_ready, b + 1)
                    load_x(b + 2, r)
                if exists(b + 1, B):
                    sp.wait_ge(hi_ready, b + 1)
                    restack(theta_hl[1 - r], 0, hi, 0, 1 - r)
                    restack(phi_hh[1 - r], 0, hi, CI, 1 - r)
                    restack(phi_hh[1 - r], CI, hi, CI, 1 - r)
                store(it, k - MT)
                if exists(b + 1, B):
                    sp.wait_ge(lo_ready, 2 * b + 2)
                    restack(theta_hl[1 - r], CI, lo, 0, 1 - r)
                    restack(phi_ll[1 - r], 0, lo, CI, 1 - r)
                    restack(phi_ll[1 - r], CI, lo, CI, 1 - r)

            image(0, 0)
            image(0, MT)
            with sp.Fori(1, B // 2 - 1) as it:
                image(it, 0)
                image(it, MT)
            image(B // 2 - 1, 0)
            image(B // 2 - 1, MT)
            store(B // 2, -2 * MT + HALF_TILES)
            store(B // 2, -MT)
            for n, piece in enumerate(LAST_PIECES):
                sp.wait_ge(result_ready, HALVES + n)
                cols = slice(N - BANK + piece.start, N - BANK + piece.stop)
                sp.dma_start(out_v[:, B - 1, cols], resid[1][:, cols]).then_inc(stored[1], 16)
            sp.wait_ge(stored[0], 16 * HALVES // 2)
            sp.wait_ge(stored[1], 16 * (HALVES // 2 + 1))

        @block.gpsimd
        def _(pool):
            nc.gpsimd.memset(ident[:, :], 0.0).then_inc(ident_zero, 1)
            pool.wait_ge(ident_zero, 1)
            nc.gpsimd.affine_select(out=ident[:, :], in_=ident[:, :], compare_op=ALU.not_equal, fill=1.0,
                                    base=0, pattern=[[-1, P]], channel_multiplier=1).then_inc(ident_ready, 1)

            level = pool.alloc_register("level")

            def hold(semaphore, value):
                if not isinstance(value, int):
                    pool.reg_mov(level, value)
                    pool.wait_ge(ident_ready, 1)
                    pool.wait_ge(semaphore, level)
                elif value > 0:
                    pool.wait_ge(semaphore, value)

            def step(it, k):
                b, j, r = image_at(it, k), k % MT, k // MT % 2
                t = tile_at(it, k - 1)
                if exists(t, TILES):
                    p = probs[(k - 1) % PROB_RING]
                    at = (k - 1) % STEPS
                    hold(inv_sum_ready, t + 1)
                    nc.gpsimd.tensor_scalar(out=p[:, :], in0=p[:, :], scalar1=inv_sum[:, at:at + 1],
                                            scalar2=1.0, op0=ALU.mult, op1=ALU.mult).then_inc(probs_scaled, 1)
                if tile_is(it, k, 1):
                    spread_peak(0, 0)
                if j == 0 and exists(b, B) and not is_first(b):
                    hold(g_factor_ready, b + 1)
                    nc.gpsimd.tensor_scalar(out=g_parts[r][:, :, 0:CI], in0=g_raw[:, :, :],
                                            scalar1=g_factor[:, r:r + 1], scalar2=1.0,
                                            op0=ALU.mult, op1=ALU.mult).then_inc(g_hi_ready, 1)
                    nc.gpsimd.tensor_scalar(out=g_scaled[:, :, :], in0=g_raw[:, :, :],
                                            scalar1=g_factor[:, r:r + 1], scalar2=1.0,
                                            op0=ALU.mult, op1=ALU.mult).then_inc(g_scaled_ready, 1)
                if j == 1 and exists(b, B) and not is_first(b):
                    hold(g_hi_ready, b + 1)
                    hold(g_scaled_ready, b)
                    nc.gpsimd.tensor_tensor(g_parts[r][:, :, CI:2 * CI], g_scaled[:, :, :],
                                            g_parts[r][:, :, 0:CI], ALU.subtract).then_inc(g_split, 1)
                if j == 2 and exists(b + 1, B):
                    hold(proj_out, 2 * b + 2)
                    if not is_first(b):
                        hold(stacked[r], it * 16 * STACKS + 16 * STACKS * ((k // MT + 1) // 2))
                    nc.gpsimd.tensor_scalar(out=hi[:, :], in0=qk[:, :], scalar1=1.0, scalar2=0.0,
                                            op0=ALU.mult, op1=ALU.add).then_inc(hi_ready, 1)
                if j in (3, 4) and exists(b + 1, B):
                    cols = slice((j - 3) * BANK, (j - 2) * BANK)
                    hold(hi_ready, b + 1)
                    nc.gpsimd.tensor_tensor(lo[:, cols], qk[:, cols], hi[:, cols].bitcast(F32),
                                            ALU.subtract).then_inc(lo_ready, 1)
                if j == 5 and exists(b + 2, B):
                    hold(g_ready, b + 2)
                    split_x(it * 16 + 16 * (k // STEPS + 2), r, 0)
                if j in (6, 7) and exists(b + 2, B):
                    split_x(b + 2, r, j - 5)
                if j == 1 and exists(b, B):
                    hold(shift_ready, 1)
                    for c in range(PER_IMAGE):
                        hold(x_arrived[r][c], it * 16 + 16 * (k // STEPS + 1))
                    hold(stored[r], it * 16 * PER_IMAGE + 16 * PER_IMAGE * (k // STEPS))
                    nc.gpsimd.tensor_scalar(out=resid[r][:, :], in0=x_in[r][:, :], scalar1=SHIFT, scalar2=1.0,
                                            op0=ALU.add, op1=ALU.mult).then_inc(resid_ready, 1)
                if j == 7 and exists(b + 1, B):
                    spread_peak(b + 1, 1 - r)

            def split_x(count, r, part):
                if part == 0:
                    for c in range(PER_IMAGE):
                        hold(x_arrived[r][c], count)
                    nc.gpsimd.tensor_scalar(out=x_hi[:, :], in0=x_in[r][:, :], scalar1=1.0, scalar2=0.0,
                                            op0=ALU.mult, op1=ALU.add).then_inc(x_hi_ready, 1)
                else:
                    cols = slice((part - 1) * BANK, part * BANK)
                    hold(x_hi_ready, count)
                    nc.gpsimd.tensor_tensor(x_lo[:, cols], x_in[r][:, cols], x_hi[:, cols].bitcast(F32),
                                            ALU.subtract).then_inc(x_lo_ready, 1)

            def spread_peak(b, r):
                hold(g_peak_ready, b + 1)
                nc.gpsimd.partition_all_reduce(g_peak_all[:, r:r + 1], g_peak[:, r:r + 1], P,
                                               bass.bass_isa.ReduceOp.max).then_inc(g_peak_everywhere, 1)

            theta_phi = w_tp[:, CI:3 * CI]
            pool.wait_ge(w_tp_in, 16)
            nc.gpsimd.tensor_scalar(out=w_tp_hi[:, :], in0=theta_phi, scalar1=1.0, scalar2=0.0,
                                    op0=ALU.mult, op1=ALU.add).then_inc(w_hi_ready, 1)
            pool.wait_ge(w_hi_ready, 1)
            nc.gpsimd.tensor_tensor(w_tp_lo[:, :], theta_phi, w_tp_hi[:, :].bitcast(F32),
                                    ALU.subtract).then_inc(w_lo_ready, 1)
            split_x(16, 1, 0)
            split_x(1, 1, 1)
            split_x(1, 1, 2)
            run_steps(pool, step, head=STEPS)

        @block.scalar
        def _(act):
            def evacuate_g(b, source, target):
                wait(act, g_split, b)
                nc.scalar.activation(target, source, ACT.Copy).then_inc(g_out, 1)

            def scale_y(h, r, source, cols):
                act.wait_ge(y_ready, h + 1)
                nc.scalar.activation(y_norm[:, cols], source, ACT.Copy,
                                     scale=y_unit[:, r:r + 1]).then_inc(y_scaled, 1)

            act.dma_start(w_tp[:, :], w_tp_t).then_inc(w_tp_in, 16)
            act.dma_start(vec[:, :], channel_vectors).then_inc(vectors_in, 16)
            act.wait_ge(bn_step, 1)
            nc.scalar.activation(STD, VAR_EPS, ACT.Sqrt).then_inc(bn_std, 1)
            act.wait_ge(bn_std, 1)
            nc.scalar.activation(table_probe[:, :], STD, ACT.Exp)
            for n, (is_phi, cols, projected) in enumerate(first_order):
                target, bias = ((theta_hl[0], BIAS_TT), (phi_hh[0], BIAS_PP))[is_phi]
                act.wait_ge(first_proj, n + 1)
                nc.scalar.activation(target[:, cols], projected, ACT.Identity,
                                     bias=bias).then_inc(first_hi, 1)
            act.wait_ge(g_ready, 1)
            evacuate_g(0, ps_flip[0][:, :], g_raw[:, :, :].rearrange("p t c -> p (t c)"))

            def step(it, k):
                image, j = image_at(it, k), k % MT
                if j in (1, 2) and exists(image + 1, B):
                    c = j - 1
                    act.wait_ge(proj_ready, 2 * image + c + 1)
                    wait(act, lo_ready, 2 * image)
                    nc.scalar.activation(qk[:, c * BANK:(c + 1) * BANK], ps_misc[:, :], ACT.Identity,
                                         bias=BIAS_TP).then_inc(proj_out, 1)
                h = half_at(it, k - 10)
                if j % HALF_TILES == 2 and exists(h, HALVES - 2):
                    act.wait_ge(y_unit_ready, image_at(it, k - 10) + 1)
                    scale_y(h, (k - 10) // MT % 2, ps_y[:, :], slice(0, BANK))
                if tile_is(it, k, TILES + 1):
                    scale_y(HALVES - 2, 1, ps_y[:, :], slice(0, BANK))
                if j == 4 and exists(image + 1, B):
                    act.wait_ge(g_ready, image + 2)
                    nc.scalar.activation(g_channels[:, :], ps_misc[:, :], ACT.Copy).then_inc(g_channels_out, 1)
                if j == 5 and exists(image + 1, B):
                    act.wait_ge(g_flipped, image + 1)
                    evacuate_g(image + 1, ps_misc[:, :].rearrange("p (a c i) -> p a c i", c=PER_IMAGE, i=CI),
                               g_raw[:, :, :].rearrange("p (c a) i -> p a c i", c=PER_IMAGE))
                t = tile_at(it, k - 2)
                if exists(t, TILES):
                    slot, ring = (k - 2) % HALF_TILES, (k - 2) // HALF_TILES % 2
                    if slot == 0:
                        wait(act, y_ready, half_at(it, k - 2) - 1)
                    for c in range(2):
                        act.wait_ge(flipped, 2 * t + c + 1)
                        nc.scalar.activation(
                            pt_hi[ring][:, c * HALF_TILES:(c + 1) * HALF_TILES, slot * P:(slot + 1) * P],
                            ps_flip[c][:, :].rearrange("p (a n) -> p a n", n=P),
                            ACT.Copy, scale=PROB_SCALE).then_inc(pt_hi_ready, 1)
                t = tile_at(it, k)
                if exists(t, TILES):
                    act.wait_ge(max_ready, t + 1)
                    wait(act, flipped, 2 * (t - PROB_RING) + 2)
                    nc.scalar.activation(probs[k % PROB_RING][:, :], ps_scores[k % 2][:, :], ACT.Exp,
                                         bias=neg_max[:, k % STEPS:k % STEPS + 1],
                                         accum_out=row_sum[:, k % STEPS:k % STEPS + 1]).then_inc(probs_ready, 1)

            run_steps(act, step)
            act.wait_ge(conv_ready, HALVES - 1)
            scale_y(HALVES - 1, 1, ps_y[:, LAST_PIECES[0]], LAST_PIECES[0])
            scale_y(HALVES, 1, ps_scores[0][:, 0:P], LAST_PIECES[1])

        @block.vector
        def _(dve):
            nc.vector.memset(warm[:, :], 0.0).then_inc(warm_ready, 1)
            dve.wait_ge(vectors_in, 16)
            nc.vector.tensor_scalar(out=VAR_EPS, in0=VAR, scalar1=EPS, scalar2=None,
                                    op0=ALU.add).then_inc(bn_step, 1)
            dve.wait_ge(bn_std, 1)
            nc.vector.reciprocal(RSTD, STD).then_inc(bn_step, 1)
            dve.wait_ge(bn_step, 2)
            nc.vector.tensor_tensor(INV, GAMMA, RSTD, ALU.mult).then_inc(bn_step, 1)
            dve.wait_ge(bn_step, 3)
            nc.vector.tensor_tensor(MEAN_INV, MEAN, INV, ALU.mult).then_inc(bn_step, 1)
            dve.wait_ge(bn_step, 4)
            nc.vector.tensor_tensor(BETA_SHIFT, BETA, MEAN_INV, ALU.subtract).then_inc(bn_step, 1)
            for n, (is_phi, cols, projected) in enumerate(first_order):
                high, target, bias, rows = ((theta_hl[0], theta_hl[0], BIAS_TT, slice(CI, P)),
                                            (phi_hh[0], phi_ll[0], BIAS_PP, slice(0, P)))[is_phi]
                dve.wait_ge(first_hi, n + 1)
                nc.vector.scalar_tensor_tensor(out=target[rows, cols], in0=projected[rows, :],
                                               scalar=bias[rows, :], in1=high[rows, cols].bitcast(F32),
                                               op0=ALU.add, op1=ALU.subtract).then_inc(first_lo, 1)

            def peak_of_g(b, r):
                dve.wait_ge(g_out, b + 1)
                wait(dve, g_peak_everywhere, b - 1)
                nc.vector.tensor_reduce(out=g_peak[:, r:r + 1], in_=g_raw[:, :, :], op=ALU.max, axis=AX.XY,
                                        apply_absolute_value=True).then_inc(g_peak_ready, 1)

            def row_maximum(t, k):
                dve.wait_ge(scores_ready, t + 1)
                nc.vector.tensor_reduce(out=neg_max[:, k % STEPS:k % STEPS + 1], in_=ps_scores[k % 2][:, :],
                                        op=ALU.max, axis=AX.X, negate=True).then_inc(max_ready, 1)

            def add_residual(h, target, source):
                dve.wait_ge(conv_ready, h + 1)
                nc.vector.scalar_tensor_tensor(out=target, in0=source, scalar=INV, in1=target,
                                               op0=ALU.mult, op1=ALU.add).then_inc(result_ready, 1)

            row_maximum(0, 0)
            dve.wait_ge(g_bias_ready, 1)
            nc.vector.tensor_tensor(BIAS_SUM, ps_flip[1][:, 0:1], B_OUT, ALU.add).then_inc(bn_step, 1)
            dve.wait_ge(bn_step, 6)
            nc.vector.scalar_tensor_tensor(out=SHIFT, in0=BIAS_SUM, scalar=INV, in1=BETA_SHIFT,
                                           op0=ALU.mult, op1=ALU.add).then_inc(shift_ready, 1)

            def step(it, k):
                image, j = image_at(it, k), k % MT
                t = tile_at(it, k - 1)
                if exists(t, TILES):
                    at = (k - 1) % STEPS
                    dve.wait_ge(probs_ready, t + 1)
                    nc.vector.reciprocal(inv_sum[:, at:at + 1],
                                         row_sum[:, at:at + 1]).then_inc(inv_sum_ready, 1)
                h = half_at(it, k - 11)
                if j % HALF_TILES == 3 and exists(h, HALVES - 2):
                    ring, part = (k - 11) // MT % 2, (k - 11) // HALF_TILES % PER_IMAGE
                    dve.wait_ge(resid_ready, image_at(it, k - 11) + 1)
                    add_residual(h, resid[ring][:, part * BANK:(part + 1) * BANK], ps_misc[:, :])
                if tile_is(it, k, 1):
                    peak_of_g(0, 0)
                if j == 6 and exists(image + 1, B):
                    peak_of_g(image + 1, (k // MT + 1) % 2)
                if j == (2 if is_first(image) else 0) and exists(image, B):
                    r = k // MT % 2
                    dve.wait_ge(g_peak_everywhere, image + 1)
                    nc.vector.tensor_scalar(out=g_unit[:, r:r + 1], in0=g_peak_all[:, r:r + 1],
                                            scalar1=G_LEAST, scalar2=1.0 / G_TOP,
                                            op0=ALU.max, op1=ALU.mult).then_inc(g_unit_ready, 1)
                    dve.wait_ge(g_unit_ready, image + 1)
                    nc.vector.reciprocal(g_factor[:, r:r + 1], g_unit[:, r:r + 1]).then_inc(g_factor_ready, 1)
                    nc.vector.tensor_scalar(out=y_unit[:, r:r + 1], in0=g_unit[:, r:r + 1],
                                            scalar1=1.0 / PROB_SCALE, scalar2=None,
                                            op0=ALU.mult).then_inc(y_unit_ready, 1)
                if tile_is(it, k, 2):
                    dve.wait_ge(g_factor_ready, 1)
                    nc.vector.tensor_scalar(out=g_parts[0][:, :, 0:CI], in0=g_raw[:, :, :],
                                            scalar1=g_factor[:, 0:1], scalar2=None,
                                            op0=ALU.mult).then_inc(g_hi_ready, 1)
                if tile_is(it, k, 3):
                    dve.wait_ge(g_hi_ready, 1)
                    nc.vector.scalar_tensor_tensor(out=g_parts[0][:, :, CI:2 * CI], in0=g_raw[:, :, :],
                                                   scalar=g_factor[:, 0:1], in1=g_parts[0][:, :, 0:CI],
                                                   op0=ALU.mult, op1=ALU.subtract).then_inc(g_split, 1)
                t = tile_at(it, k - 2)
                if exists(t, TILES):
                    slot, ring = (k - 2) % HALF_TILES, (k - 2) // HALF_TILES % 2
                    for c in range(2):
                        where = (slice(None), slice(c * HALF_TILES, (c + 1) * HALF_TILES),
                                 slice(slot * P, (slot + 1) * P))
                        dve.wait_ge(pt_hi_ready, 2 * t + c + 1)
                        nc.vector.scalar_tensor_tensor(
                            out=pt_lo[ring][where], in0=ps_flip[c][:, :].rearrange("p (a n) -> p a n", n=P),
                            scalar=PROB_SCALE, in1=pt_hi[ring][where],
                            op0=ALU.mult, op1=ALU.subtract).then_inc(pt_lo_ready, 1)
                t = tile_at(it, k + 1)
                if exists(t, TILES):
                    row_maximum(t, k + 1)

            run_steps(dve, step)
            dve.wait_ge(resid_ready, B)
            add_residual(HALVES - 2, resid[1][:, 0:BANK], ps_misc[:, :])
            add_residual(HALVES - 1, resid[1][:, BANK:N - P], ps_scores[1][:, 0:BANK - P])
            add_residual(HALVES, resid[1][:, N - P:N], ps_scores[0][:, BANK:BANK + P])

        @block.tensor
        def _(pe):
            def first_g(tiles):
                for m in tiles:
                    last = nc.tensor.matmul(ps_flip[0][:, m * CI:(m + 1) * CI], x_in[0][:, m * P:(m + 1) * P],
                                            wg[:, :], start=True, stop=True)
                return last

            def scores(t, it, k):
                r, cols = k // MT % 2, slice(k % MT * P, (k % MT + 1) * P)
                if k % MT == 0 and not (isinstance(t, int) and t == 0):
                    pe.wait_ge(stacked[r], it * 16 * STACKS + 16 * STACKS * ((k // MT + 1) // 2))
                if isinstance(t, int) and t < 2:
                    pe.wait_ge(first_lo, (NEEDED_BY_TILE_0, len(first_order))[t])
                wait(pe, probs_ready, t - 1)
                for n, phi in enumerate((phi_hh[r], phi_ll[r])):
                    for c in range(PER_IMAGE):
                        cc = slice(c * BANK, (c + 1) * BANK)
                        last = nc.tensor.matmul(ps_scores[k % 2][:, cc], theta_hl[r][:, cols], phi[:, cc],
                                                start=(n == 0), stop=(n == 1))
                last.then_inc(scores_ready, 1)

            def weighted_sum(quarters, ring, r, target, to, cols):
                g = g_parts[r]
                for quarter in quarters:
                    for m in (2 * quarter, 2 * quarter + 1):
                        nc.tensor.matmul(target[:, to], g[:, m, :], pt_hi[ring][:, m, cols],
                                         start=(m == 0), stop=False, skip_group_check=True)
                    for side in range(2):
                        m = 2 * quarter + side
                        last = nc.tensor.matmul(target[side * CI:(side + 1) * CI, to], g[:, m, 0:CI],
                                                pt_lo[ring][:, m, cols], start=False, stop=(m >= MT - 2),
                                                skip_group_check=True)
                if quarters[-1] == HALF_TILES - 1:
                    last.then_inc(y_ready, 1)

            def convolve(h, target, cols):
                pe.wait_ge(y_scaled, h + 1)
                nc.tensor.matmul(target, wout[:, 0:C], y_norm[:, cols],
                                 start=True, stop=True).then_inc(conv_ready, 1)

            pe.wait_ge(warm_ready, 1)
            for _ in range(WARM_UP):
                nc.tensor.matmul(ps_y[:, 0:P], warm[:, :], warm[:, :], start=True, stop=True)

            pe.wait_ge(w_tp_in, 16)
            for is_phi, cols, projected in first_order:
                pe.wait_ge(x_arrived[0][cols.start // BANK], 16)
                nc.tensor.matmul(projected, w_tp[:, 2 * CI * is_phi:2 * CI * (is_phi + 1)],
                                 x_in[0][:, cols], start=True, stop=True).then_inc(first_proj, 1)
            pe.wait_ge(w_g_in, 16)
            first_g(range(MT // 2))
            scores(0, 0, 0)
            first_g(range(MT // 2, MT)).then_inc(g_ready, 1)
            pe.wait_ge(w_out_in, 32)
            nc.tensor.matmul(ps_flip[1][:, 0:1], wout[0:CI, 0:C], wout[0:CI, C:C + 1],
                             start=True, stop=True).then_inc(g_bias_ready, 1)
            pe.wait_ge(ident_ready, 1)

            def step(it, k):
                image, j = image_at(it, k), k % MT
                t = tile_at(it, k - 2)
                if exists(t, TILES):
                    pe.wait_ge(probs_scaled, t + 1)
                    for c in range(2):
                        if isinstance(t, int) and t == 0:
                            pe.wait_ge(*((g_out, 1), (shift_ready, 1))[c])
                        wait(pe, pt_lo_ready, 2 * t + c - 1)
                        for a in range(HALF_TILES):
                            m = c * HALF_TILES + a
                            last = nc.tensor.transpose(ps_flip[c][:, a * P:(a + 1) * P],
                                                       probs[(k - 2) % PROB_RING][:, m * P:(m + 1) * P],
                                                       ident[:, :])
                        last.then_inc(flipped, 1)

                t = tile_at(it, k + 1)
                if exists(t, TILES):
                    scores(t, it, k + 1)

                image, j = image_at(it, k), k % MT
                more = exists(image + 1, B)
                if j in (0, 1) and more:
                    if j == 0:
                        if isinstance(image, int) and image == 0:
                            pe.wait_ge(w_lo_ready, 1)
                        pe.wait_ge(x_lo_ready, 2 * image + 2)
                    else:
                        pe.wait_ge(proj_out, 2 * image + 1)
                    cols = slice(j * BANK, (j + 1) * BANK)
                    for n, (w, xs) in enumerate(((w_tp_hi, x_hi), (w_tp_lo, x_hi), (w_tp_hi, x_lo))):
                        last = nc.tensor.matmul(ps_misc[:, :], w[:, :], xs[:, cols],
                                                start=(n == 0), stop=(n == 2))
                    last.then_inc(proj_ready, 1)
                h = half_at(it, k - 10)
                if j % HALF_TILES == 2 and exists(h, HALVES - 2):
                    if more:
                        pe.wait_ge(*((proj_out, 2 * image + 2) if j == 2 else (g_out, image + 2)))
                    else:
                        wait(pe, result_ready, h)
                    convolve(h, ps_misc[:, :], slice(0, BANK))
                if j == 3 and more:
                    wait(pe, proj_out, 2 * image + 2)
                    wait(pe, result_ready, 2 * image - 1)
                    for c in range(PER_IMAGE):
                        last = nc.tensor.matmul(ps_misc[c * CI:(c + 1) * CI, :], wg[:, :],
                                                x_in[(k // MT + 1) % 2][:, c * BANK:(c + 1) * BANK],
                                                start=True, stop=True, skip_group_check=True)
                    last.then_inc(g_ready, 1)
                if j == 4 and more:
                    pe.wait_ge(g_channels_out, image + 1)
                    for a in range(HALF_TILES):
                        last = nc.tensor.transpose(ps_misc[:, a * P:(a + 1) * P],
                                                   g_channels[:, a * P:(a + 1) * P], ident[:, :])
                    last.then_inc(g_flipped, 1)

                h, quarter = half_at(it, k - 6), (k - 6) % HALF_TILES
                if exists(h, HALVES - 2):
                    if quarter == 0:
                        pe.wait_ge(pt_lo_ready, 2 * HALF_TILES * h + 2 * HALF_TILES)
                        pe.wait_ge(g_split, image_at(it, k - 6) + 1)
                        wait(pe, y_scaled, h)
                    weighted_sum((quarter,), (k - 6) // HALF_TILES % 2, (k - 6) // MT % 2,
                                 ps_y, slice(0, BANK), slice(0, BANK))
                if tile_is(it, k, TILES - 2):
                    pe.wait_ge(pt_lo_ready, 2 * (TILES - HALF_TILES))
                    pe.wait_ge(g_split, B)
                    pe.wait_ge(y_scaled, HALVES - 2)
                for tile, quarters in ((TILES - 2, (0,)), (TILES - 1, (1, 2)), (TILES, (3,))):
                    if tile_is(it, k, tile):
                        weighted_sum(quarters, 0, 1, ps_y, slice(0, BANK), slice(0, BANK))

            run_steps(pe, step)
            whole = tuple(range(HALF_TILES))
            pe.wait_ge(result_ready, HALVES - 2)
            convolve(HALVES - 2, ps_misc[:, :], slice(0, BANK))
            pe.wait_ge(pt_lo_ready, 2 * TILES - 2)
            weighted_sum(whole, 1, 1, ps_y, LAST_PIECES[0], LAST_PIECES[0])
            pe.wait_ge(pt_lo_ready, 2 * TILES)
            pe.wait_ge(probs_ready, TILES)
            weighted_sum(whole, 1, 1, ps_scores[0], slice(0, P), LAST_PIECES[1])
            convolve(HALVES - 1, ps_scores[1][:, 0:BANK - P], LAST_PIECES[0])
            convolve(HALVES, ps_scores[0][:, BANK:BANK + P], LAST_PIECES[1])


def kernel(x, L0_conv_w_g, L0_conv_b_g, L0_conv_w_theta, L0_conv_b_theta, L0_conv_w_phi, L0_conv_b_phi,
           L0_conv_w_out, L0_conv_b_out, L0_conv_bn_gamma, L0_conv_bn_beta, L0_conv_bn_mean, L0_conv_bn_var):
    import concourse.bacc as bacc
    import numpy as np
    from concourse import mybir
    from concourse.bass_utils import run_bass_kernel_spmd

    def rows(*parts):
        return np.ascontiguousarray(np.stack([np.asarray(p) for p in parts], axis=1))

    theta, phi = np.asarray(L0_conv_w_theta), np.asarray(L0_conv_w_phi)
    w_tp_t = np.ascontiguousarray(np.concatenate([theta, theta, phi, phi]).T)
    w_g_t = np.ascontiguousarray(np.asarray(L0_conv_w_g).T)
    w_out_t = np.ascontiguousarray(np.concatenate([np.asarray(L0_conv_w_out).T,
                                                   np.asarray(L0_conv_b_g)[:, None]], axis=1))
    b_theta, b_phi = np.asarray(L0_conv_b_theta), np.asarray(L0_conv_b_phi)
    vectors = rows(np.concatenate([b_theta, b_phi]), np.concatenate([b_theta, b_theta]),
                   np.concatenate([b_phi, b_phi]), L0_conv_b_out, L0_conv_bn_gamma,
                   L0_conv_bn_beta, L0_conv_bn_mean, L0_conv_bn_var)
    arrays = {"x_in_dram": np.ascontiguousarray(x), "w_tp_t_dram": w_tp_t, "w_g_t_dram": w_g_t,
              "w_out_t_dram": w_out_t, "vectors_dram": vectors}
    nc = bacc.Bacc("TRN2", target_bir_lowering=False, num_devices=1)
    args = [nc.dram_tensor(name, a.shape, mybir.dt.from_np(a.dtype), kind="ExternalInput").ap()
            for name, a in arrays.items()]
    shape = arrays["x_in_dram"].shape
    out = nc.dram_tensor("out_dram", shape, mybir.dt.float32, kind="ExternalOutput").ap()
    build_nonlocal_attention(nc, *args, out)
    return run_bass_kernel_spmd(nc, [arrays], core_ids=[0]).results[0]["out_dram"]
```
